# Optimizing a Trainium2 kernel written in Bass

```python
import numpy as np
import jax
import jax.numpy as jnp

def _softmax(x, axis=-1):
    return jax.nn.softmax(x, axis=axis)

def _gelu(x):
    return jax.nn.gelu(x, approximate=True)

def _silu(x):
    return jax.nn.silu(x)

def _sigmoid(x):
    return jax.nn.sigmoid(x)

def _layernorm(x, axis=-1, eps=1e-05):
    m = jnp.mean(x, axis=axis, keepdims=True)
    v = jnp.var(x, axis=axis, keepdims=True)
    return (x - m) / jnp.sqrt(v + eps)

def _scatter_add(tgt, idx, src, axis=0):
    return tgt.at[idx].add(src)

def _segment_sum(src, seg, n):
    return jax.ops.segment_sum(src, seg, n)
kernel_name = 'mk_adaln_d1_jaxref_r8_b0c581'

def setup_inputs(seed: int=0):
    np.random.seed(seed)
    _w = jnp.asarray

    def _L0_attn_setup():
        import jax, jax.numpy as jnp
        import numpy as np
        D = 128
        H = 16
        HD = D // H
        B = 2
        T = 256

        def _apply_rotary(x, rope):
            x1, x2 = (x[..., ::2], x[..., 1::2])
            sin, cos = (rope[..., ::2], rope[..., 1::2])
            return jnp.concatenate([x1 * cos - x2 * sin, x1 * sin + x2 * cos], axis=-1)
        key = jax.random.key(seed)
        k0, k1, k2 = jax.random.split(key, 3)
        s = 1.0 / np.sqrt(D)
        return {'x': jax.random.normal(k0, (B, T, D), dtype=jnp.float32), 'qkv_w': jax.random.normal(k1, (D, 3 * D), dtype=jnp.float32) * s, 'qkv_b': jnp.zeros((3 * D,), dtype=jnp.float32), 'out_w': jax.random.normal(k2, (D, D), dtype=jnp.float32) * s, 'out_b': jnp.zeros((D,), dtype=jnp.float32)}
    _L0_attn_in = _L0_attn_setup()

    def _L0_ffn_setup():
        import jax, jax.numpy as jnp
        import numpy as np
        DIM = 128
        MLP_MULT = 4
        NUM_EXPERTS = 8
        EXPERT_HIDDEN = MLP_MULT * DIM // NUM_EXPERTS
        key = jax.random.key(seed)
        k_x, k_r, k_fc, k_pj = jax.random.split(key, 4)
        x = jax.random.normal(k_x, (4, 512, DIM), dtype=jnp.float32)
        w_router = jax.random.normal(k_r, (NUM_EXPERTS, DIM), dtype=jnp.float32) * (1.0 / np.sqrt(DIM))
        w_fc = jax.random.normal(k_fc, (NUM_EXPERTS, EXPERT_HIDDEN, DIM), dtype=jnp.float32) * (1.0 / np.sqrt(DIM))
        w_proj = jax.random.normal(k_pj, (NUM_EXPERTS, DIM, EXPERT_HIDDEN), dtype=jnp.float32) * (1.0 / np.sqrt(EXPERT_HIDDEN))
        return {'x': x, 'w_router': w_router, 'w_fc': w_fc, 'w_proj': w_proj}
    _L0_ffn_in = _L0_ffn_setup()
    _L0_c = _w((lambda *s: np.random.randn(*s).astype(np.float32) * 0.05)(2, 128))
    _L0_wmod = _w((lambda *s: np.random.randn(*s).astype(np.float32) * 0.05)(128, 6 * 128) * 128 ** (-0.5))
    _d = {'L0_attn_x': _L0_attn_in['x'], 'L0_attn_qkv_w': _L0_attn_in['qkv_w'], 'L0_attn_qkv_b': _L0_attn_in['qkv_b'], 'L0_attn_out_w': _L0_attn_in['out_w'], 'L0_attn_out_b': _L0_attn_in['out_b'], 'L0_ffn_w_router': _L0_ffn_in['w_router'], 'L0_ffn_w_fc': _L0_ffn_in['w_fc'], 'L0_ffn_w_proj': _L0_ffn_in['w_proj'], 'L0_c': _L0_c, 'L0_wmod': _L0_wmod}
    _x0 = _d['L0_attn_x']
    _d['L0_attn_x'] = jax.random.normal(jax.random.fold_in(jax.random.key(seed), 1), (2, 1024, 128), dtype=_x0.dtype)
    del _x0
    return _d

def reference(L0_attn_x, L0_attn_qkv_w, L0_attn_qkv_b, L0_attn_out_w, L0_attn_out_b, L0_ffn_w_router, L0_ffn_w_fc, L0_ffn_w_proj, L0_c, L0_wmod):

    def _L0_attn_ref(x, qkv_w, qkv_b, out_w, out_b):
        import jax, jax.numpy as jnp
        import numpy as np
        D = 128
        H = 16
        HD = D // H
        B = 2
        T = 256

        def _apply_rotary(x, rope):
            x1, x2 = (x[..., ::2], x[..., 1::2])
            sin, cos = (rope[..., ::2], rope[..., 1::2])
            return jnp.concatenate([x1 * cos - x2 * sin, x1 * sin + x2 * cos], axis=-1)
        Bx, Tx, Dm = x.shape
        qkv = (x @ qkv_w + qkv_b).reshape(Bx, Tx, 3, H, HD).transpose(2, 0, 3, 1, 4)
        q, k, v = (qkv[0], qkv[1], qkv[2])
        inv_freq = 1.0 / 10000.0 ** (jnp.arange(0, HD, 2, dtype=jnp.float32) / HD)
        t = jnp.arange(Tx, dtype=jnp.float32)
        freqs = t[:, None] * inv_freq[None, :]
        rope = jnp.concatenate([jnp.sin(freqs), jnp.cos(freqs)], axis=-1)
        q = _apply_rotary(q, rope)
        k = _apply_rotary(k, rope)
        scale = HD ** (-0.5)
        scores = jnp.einsum('bhqd,bhkd->bhqk', q, k) * scale
        causal_mask = jnp.triu(jnp.ones((Tx, Tx), dtype=bool), 1)
        scores = jnp.where(causal_mask, -jnp.inf, scores)
        attn = jax.nn.softmax(scores, axis=-1)
        out = jnp.einsum('bhqk,bhkd->bhqd', attn, v)
        out = out.transpose(0, 2, 1, 3).reshape(Bx, Tx, Dm)
        return out @ out_w + out_b

    def _L0_ffn_ref(x, w_router, w_fc, w_proj):
        import jax, jax.numpy as jnp
        import numpy as np
        DIM = 128
        MLP_MULT = 4
        NUM_EXPERTS = 8
        EXPERT_HIDDEN = MLP_MULT * DIM // NUM_EXPERTS
        logits = jnp.einsum('bsd,ed->bse', jax.lax.stop_gradient(x), w_router)
        weights = jax.nn.softmax(logits, axis=-1)
        indices = jnp.argmax(weights, axis=-1)
        onehot = jax.nn.one_hot(indices, NUM_EXPERTS, dtype=x.dtype)
        h = jnp.einsum('bsd,ehd->bseh', x, w_fc)
        h = jnp.where(h >= 0, h, 0.5 * h)
        h = h * h
        out = jnp.einsum('bseh,edh,bse->bsd', h, w_proj, onehot)
        return out
    x = L0_attn_x
    mod = (_silu(L0_c) @ L0_wmod).reshape(L0_c.shape[0], 6, 1, -1)
    sa, ca, ga, sb, cb, gb = (mod[:, 0], mod[:, 1], mod[:, 2], mod[:, 3], mod[:, 4], mod[:, 5])
    ga = (2 * (ga >= 0) - 1) * jnp.maximum(jnp.abs(ga), 0.25)
    gb = (2 * (gb >= 0) - 1) * jnp.maximum(jnp.abs(gb), 0.25)
    h = _layernorm(x, axis=-1) * (1 + ca) + sa
    x = x + ga * _L0_attn_ref(h, L0_attn_qkv_w, L0_attn_qkv_b, L0_attn_out_w, L0_attn_out_b)
    h = _layernorm(x, axis=-1) * (1 + cb) + sb
    x = x + gb * _L0_ffn_ref(h, L0_ffn_w_router, L0_ffn_w_fc, L0_ffn_w_proj)
    return x

_drawn_inputs = setup_inputs


def setup_inputs(seed=0):
    import zlib

    import numpy as np

    out = dict(_drawn_inputs(seed))
    spreads = {'L0_attn_qkv_b': (0.0, 0.1), 'L0_attn_out_b': (0.0, 0.1)}
    factors = {}
    for name, (base, spread) in spreads.items():
        noise = np.random.default_rng([zlib.crc32(name.encode()), seed]).standard_normal(out[name].shape)
        drawn = base * np.exp(spread * noise) if base else spread * noise
        out[name] = jnp.asarray(drawn.astype(out[name].dtype))
    for name, factor in factors.items():
        out[name] = (out[name] * factor).astype(out[name].dtype)
    return out
```

```python
from contextlib import ExitStack

import concourse.bass as bass
from concourse import mybir

ALU = mybir.AluOpType
ACT = mybir.ActivationFunctionType
AX = mybir.AxisListType
F32 = mybir.dt.float32
BF16 = mybir.dt.bfloat16
I32 = mybir.dt.int32

P = 128
B, T, D = 2, 1024, 128
H = 16
HD = D // H
NE, EH = 8, 64
HID = NE * EH
HALF = T // 2
TU = HALF // P
HG = 4
NG = H // HG
PARTS = 3
ROWS = PARTS * PARTS * HD
ROWSM = ROWS + PARTS
VW = HD + 1
VPAD = H * VW + 24
SCALE = float(HD) ** -0.5
EPS = 1e-5
ONES = 1 + 0x3F80 / 2 ** 23
LOW = -(2.0 ** 127)

UNITS = [(0, 0), (0, 1), (1, 1), (1, 0)]
PREPS = [(0, 0), (0, 1), (1, 0), (1, 1)]
STEPS = [(b, half, g) for b, half in UNITS for g in range(NG)]


def bank_jobs_a(half):
    jobs = []
    for r in range(TU):
        jobs.append(("diag", r, 0, HG, P))
        if r:
            nh = min(HG, HALF // (r * P)) if r < 3 else 1
            jobs += [("tri", r, h, nh, r * P) for h in range(0, HG, nh)]
        if half:
            jobs += [("sq", r, h, 1, HALF) for h in range(HG)]
    return jobs


def groups_b(half):
    out = []
    if half:
        out += [(kt, 0, 0, [(h, 1) for h in range(HG)]) for kt in range(TU)]
    for kt in range(TU):
        n = HALF - kt * P
        nh = max(1, HALF // n) if n < 384 else 1
        out.append((kt, half, kt * P, [(h, nh) for h in range(0, HG, nh)]))
    return out


LEAD = 9
PVLAG = 2


def plan():
    a_at, a_end, n = {}, [], 0
    for s, (b, half, g) in enumerate(STEPS):
        for job in bank_jobs_a(half):
            a_at[n] = (s, job)
            n += 1
        a_end.append(n)
    b_at, v_at, stages = {}, {}, {}
    slot, v_end = 0, []
    for s, (b, half, g) in enumerate(STEPS):
        slot = max(slot, a_end[s] + LEAD)
        for gi, grp in enumerate(groups_b(half)):
            for bank in grp[3]:
                b_at[slot] = (s, gi, grp, bank, bank is grp[3][-1])
                slot += 1
            v_at[slot - 1 + PVLAG] = (s, gi, grp)
        v_end.append(slot - 1 + PVLAG)

    def put(at, *stage):
        stages.setdefault(at, []).append(stage)

    def prep(at, u, gap):
        for i, name in enumerate(["norm1", "hT", "q1", "q2", "q3", "k1", "k2", "k3", "v"]):
            put(at + i * gap, name, u)

    for s in range(len(STEPS)):
        put(a_end[s] - 1, "max1", s)
        put(a_end[s] + 1, "max2", s)
        put(v_end[s], "o", s)
    prep(1, (0, 1), 2)
    for g in range(NG):
        put(21, "load", (0, 1), g)
    put(23, "gates", 0)
    prep(46, (1, 0), 2)
    prep(65, (1, 1), 2)
    for g in range(NG):
        for half in range(2):
            put(v_end[4 + g] + 1, "load", (1, half), g)
    for n, u in enumerate(UNITS):
        at = v_end[4 * n + 3] + 1
        names = ["xb"] + [f"n{t}" for t in range(TU)] + ["oT", "out", "ln", "h2", "rt", "ohT"] \
            + [f"f{c}" for c in range(4)] + ["y"]
        for i, name in enumerate(names):
            put(at + i * 2, name, u)
    slots = max(list(a_at) + list(b_at) + list(v_at) + list(stages)) + 1
    return slots, a_at, b_at, v_at, stages, a_end


PRE = [("mod", 0), ("norm1", (0, 0)), ("hT", (0, 0)), ("q1", (0, 0)), ("k1", (0, 0)), ("q2", (0, 0)), ("k2", (0, 0)),
       ("q3", (0, 0)), ("k3", (0, 0)), ("v", (0, 0))] + [("load", (0, 0), g) for g in range(NG)]
BANKS_OF = {"mod": 2, "hT": 1, "q1": 2, "k1": 2, "v": 1, "oT": 1, "out": 1, "h2": 1, "rt": 1, "ohT": 1, "y": 1,
            **{f"n{t}": 1 for t in range(TU)}, **{f"f{c}": 2 for c in range(4)}}


def adaln_block(nc, x, ct, wmod, wqkv, wsw, bcol, bv, wo, bo, wr, wfc, wpj, rope, out):
    slots, a_at, b_at, v_at, stages, a_end = plan()
    order = list(PRE) + [st for i in range(slots) for st in stages.get(i, [])]
    side_job, n = {}, 0
    for st in order:
        for k in range(BANKS_OF.get(st[0], 0)):
            side_job[(st[0], st[1], k)] = n
            n += 1
    group_no = {}
    for i in sorted(b_at):
        group_no.setdefault(b_at[i][0:2], len(group_no))
    bank_no = {i: n for n, i in enumerate(sorted(b_at))}
    prep_no = {u: n for n, u in enumerate(PREPS)}
    unit_no = {u: n for n, u in enumerate(UNITS)}
    qparts = nc.dram_tensor("qparts", (B * 2, H, 5, HD, HALF), BF16).ap()
    kparts = nc.dram_tensor("kparts", (B * 2, H, 3, HD, HALF), BF16).ap()

    with ExitStack() as ctx:
        def sb(name, shape, dt=F32):
            return ctx.enter_context(nc.sbuf_tensor(name, shape, dt))

        def bank(name, n=1):
            return ctx.enter_context(nc.psum_tensor(name, [P, n, HALF], F32))

        def sem(name):
            return ctx.enter_context(nc.semaphore(name))

        ct_sb = sb("ct_sb", [P, B])
        wmod_sb = sb("wmod_sb", [P, 6 * D])
        wqkv_sb = sb("wqkv_sb", [P, 3 * D])
        wsw_sb = sb("wsw_sb", [P, 2 * D])
        bcol_sb = sb("bcol_sb", [P, 4])
        bv_sb = sb("bv_sb", [P, D])
        bo_sb = sb("bo_sb", [P, D])
        wo_sb = sb("wo_sb", [P, D])
        wr_sb = sb("wr_sb", [P, NE])
        wfc_sb = sb("wfc_sb", [P, HID])
        wpj_sb = sb("wpj_sb", [P, 4, D])
        rope_sb = sb("rope_sb", [P, 2, T])
        ident = sb("ident", [P, P])
        identb = sb("identb", [P, P], BF16)
        maska = sb("maska", [P, HG, P], BF16)
        esel = sb("esel", [NE, HID], BF16)
        rank_i = sb("rank_i", [P, TU, NE], I32)
        rank = sb("rank", [P, TU, NE])
        mhalf = sb("mhalf", [P, TU])
        sig = sb("sig", [P, 3, B])
        silu = sb("silu", [P, B])
        silu_b = sb("silu_b", [P, B, P])
        modcol = sb("modcol", [P, 4, B])
        gneg = sb("gneg", [P, 2 * B * D])
        gate = sb("gate", [P, B, 2, D])
        wog = sb("wog", [P, B, D])
        bog = sb("bog", [P, B, D])
        wpg = sb("wpg", [P, B, 4, D])
        xs = sb("xs", [P, B * 2, TU, D])
        stats = sb("stats", [P, TU, 6])
        mv = sb("mv", [P, TU, 2])
        veps = sb("veps", [P, TU])
        rstd = sb("rstd", [P, TU])
        xn = sb("xn", [P, TU, D])
        ht = sb("ht", [P, HALF])
        rot = [sb(f"rot{i}", [P, 2, HALF]) for i in range(2)]
        full = [sb(f"full{i}", [P, HALF]) for i in range(2)]
        part = [sb(f"part{i}", [P, PARTS, HALF], BF16) for i in range(2)]
        qst = sb("qst", [ROWSM, 2, H, HALF], BF16)
        kst = sb("kst", [ROWSM, 2, H, HALF], BF16)
        v_sb = sb("v_sb", [P, B * 2 * TU, VPAD])
        tmax = [sb(f"tmax{i}", [P, 2, 3, TU, HG]) for i in range(2)]
        negm = sb("negm", [P, 2, HG, TU])
        negr = sb("negr", [P, HG * TU])
        negp = sb("negp", [P, 2, PARTS, HG * TU], BF16)
        negt = sb("negt", [PARTS * HG * TU, 2, P], BF16)
        NP = 3
        pt = sb("pt", [P, NP, HG, HALF])
        ot = sb("ot", [P, NG, HALF])
        rden = sb("rden", [P, NG, HG])
        on = sb("on", [P, TU, D])
        ont = sb("ont", [P, HALF])
        x2 = sb("x2", [P, TU, D])
        xn2 = sb("xn2", [P, TU, D])
        h2t = sb("h2t", [P, HALF])
        lmax = sb("lmax", [P, TU])
        leq = sb("leq", [P, TU, NE])
        onehot = sb("onehot", [P, TU, NE])
        oht = sb("oht", [NE, HALF], BF16)
        fa = sb("fa", [P, HALF])
        fm = sb("fm", [P, HALF])
        fl = sb("fl", [P, HALF])
        fg = sb("fg", [P, 4, HALF])
        y = sb("y", [P, TU, D])

        ps_a = bank("ps_a", 2)
        ps_b = bank("ps_b", 2)
        ps_o = bank("ps_o")
        ps_m = bank("ps_m")
        ps_s = bank("ps_s", 2)

        s_ldx = [sem(f"s_ldx{i}") for i in range(B * 2)]
        s_ldmod, s_ldqkv, s_ldrest = sem("s_ldmod"), sem("s_ldqkv"), sem("s_ldrest")
        s_ident, s_mask, s_consts, s_ones = sem("s_ident"), sem("s_mask"), sem("s_consts"), sem("s_ones")
        s_pool = sem("s_pool")
        s_dve = sem("s_dve")
        s_exp0, s_silu, s_gated = sem("s_exp0"), sem("s_silu"), sem("s_gated")
        s_var, s_rstd, s_xn = sem("s_var"), sem("s_rstd"), sem("s_xn")
        s_full = [sem(f"s_full{i}") for i in range(2)]
        s_part = [sem(f"s_part{i}") for i in range(2)]
        s_rem = [sem(f"s_rem{i}") for i in range(2)]
        s_store = [sem(f"s_store{i}") for i in range(2)]
        s_stack = [[sem(f"s_stack{h}_{g}") for g in range(NG)] for h in range(2)]
        s_a, s_max = sem("s_a"), sem("s_max")
        s_b, s_exp, s_tri, s_pv = sem("s_b"), sem("s_exp"), sem("s_tri"), sem("s_pv")
        s_negm, s_negp, s_mrow, s_negt = sem("s_negm"), sem("s_negp"), sem("s_mrow"), sem("s_negt")
        s_mstack = [sem(f"s_mstack{i}") for i in range(2)]
        s_ot = sem("s_ot")
        s_side = [sem(f"s_side{i}") for i in range(2)]
        s_sfree = [sem(f"s_sfree{i}") for i in range(2)]
        s_xb, s_fl, s_fg, s_out = sem("s_xb"), sem("s_fl"), sem("s_fg"), sem("s_out")

        block = ctx.enter_context(nc.Block())

        def side(st, k=0):
            j = side_job[(st[0], st[1], k)]
            return ps_s[:, j % 2, :], j % 2, j // 2

        def side_ready(eng, st, k=0):
            ap, i, use = side(st, k)
            eng.wait_ge(s_side[i], use + 1)
            return ap, s_sfree[i]

        def wait_read(eng, name, u, k=0):
            _, i, use = side((name, u), k)
            eng.wait_ge(s_sfree[i], use + 1)

        def norm_no(st):
            return [x for x in order if x[0] in ("norm1", "out")].index(st)

        @block.sync
        def _(sp):
            sp.dma_start(ct_sb[:, :], ct).then_inc(s_ldmod, 16)
            sp.dma_start(xs[:, 0], x[0]).then_inc(s_ldx[0], 16)
            sp.dma_start(wmod_sb[:, :], wmod).then_inc(s_ldmod, 16)
            sp.dma_start(wqkv_sb[:, :], wqkv).then_inc(s_ldqkv, 16)
            sp.dma_start(wsw_sb[:, :], wsw).then_inc(s_ldqkv, 16)
            sp.dma_start(bcol_sb[:, :], bcol).then_inc(s_ldqkv, 16)
            sp.dma_start(rope_sb[:, :, :], rope).then_inc(s_ldqkv, 16)
            sp.dma_start(bv_sb[:, :], bv.partition_broadcast(P)).then_inc(s_ldqkv, 16)
            for i in range(1, B * 2):
                sp.dma_start(xs[:, i], x[i]).then_inc(s_ldx[i], 16)
            sp.dma_start(bo_sb[:, :], bo.partition_broadcast(P)).then_inc(s_ldrest, 16)
            sp.dma_start(wo_sb[:, :], wo).then_inc(s_ldrest, 16)
            sp.dma_start(wr_sb[:, :], wr).then_inc(s_ldrest, 16)
            sp.dma_start(wfc_sb[:, :], wfc).then_inc(s_ldrest, 16)
            sp.dma_start(wpj_sb[:, :, :], wpj).then_inc(s_ldrest, 16)

            def store(u, i):
                n, w = prep_no[u], 2 * u[0] + u[1]
                sp.wait_ge(s_part[i], 3 * (n + 1))
                dst = (qparts, kparts)[i]
                for slot in range(5 if i == 0 else 3):
                    sp.dma_start(dst[w, :, slot], part[i][:, slot % PARTS, :]).then_inc(s_store[i], 16)

            def load(u, g):
                (b, half), w, n = u, 2 * u[0] + u[1], prep_no[u]
                sp.wait_ge(s_store[0], 5 * 16 * (n + 1))
                sp.wait_ge(s_store[1], 3 * 16 * (n + 1))
                sp.wait_ge(s_ones, 1)
                if b:
                    sp.wait_ge(s_pv, group_no[(NG + g, len(groups_b(1)) - 1)] + 1)
                h0, R = HG * g, PARTS * HD
                for i in range(PARTS):
                    q = qparts[w, h0:h0 + HG, i:i + 3].rearrange("h j d t -> (j d) h t")
                    k = kparts[w, h0:h0 + HG].rearrange("h j d t -> (j d) h t")
                    sp.dma_start(qst[R * i:R * i + R, half, h0:h0 + HG, :], q).then_inc(s_stack[half][g], 16)
                    sp.dma_start(kst[R * i:R * i + R, half, h0:h0 + HG, :], k).then_inc(s_stack[half][g], 16)

            def max_rows(s):
                b, half, g = STEPS[s]
                sp.wait_ge(s_negt, s + 1)
                M = HG * TU
                for p in range(PARTS):
                    dst = qst[ROWS + p:ROWS + p + 1, half, HG * g:HG * g + HG, :].rearrange("o h (r x) -> o (h r) x", x=P)
                    sp.dma_start(dst, negt[M * p:M * p + M, s % 2, :]).then_inc(s_mstack[s % 2], 16)

            def run(st):
                if st[0] in ("q3", "k3"):
                    store(st[1], 0 if st[0] == "q3" else 1)
                if st[0] == "load":
                    load(st[1], st[2])
                if st[0] == "max2":
                    max_rows(st[1])
                if st[0] == "y":
                    wait_read(sp, "y", st[1])
                    sp.dma_start(out[2 * st[1][0] + st[1][1]], y[:, :, :]).then_inc(s_out, 16)

            for st in order:
                run(st)
            sp.wait_ge(s_out, 16 * len(UNITS))

        @block.gpsimd
        def _(pool):
            count = [0]

            def link(ins):
                count[0] += 1
                ins.then_inc(s_pool, 1)
                pool.wait_ge(s_pool, count[0])

            link(pool.memset(mhalf[:, :], -0.5))
            link(pool.memset(ident[:, :], 0.0))
            pool.affine_select(out=ident[:, :], in_=ident[:, :], compare_op=ALU.not_equal, fill=1.0, base=0,
                               pattern=[[-1, P]], channel_multiplier=1).then_inc(s_ident, 1)

            def rest_of_consts():
                ones2 = kst[64:ROWSM].rearrange("p a h t -> p (a h t)").bitcast(F32)
                pool.wait_ge(s_rstd, 1)
                pool.memset(ones2, ONES).then_inc(s_ones, 1)
                pool.wait_ge(s_ones, 1)
                pool.wait_ge(s_ident, 1)
                link(pool.tensor_copy(identb[:, :], ident[:, :]))
                link(pool.memset(maska[:, :, :], 0.0))
                pool.affine_select(out=maska[:, :, :], in_=maska[:, :, :], compare_op=ALU.is_ge, fill=LOW, base=0,
                                   pattern=[[0, HG], [-1, P]], channel_multiplier=1).then_inc(s_mask, 1)
                link(pool.memset(v_sb[:, :, :], 1.0))
                link(pool.memset(esel[:, :], 1.0))
                link(pool.affine_select(out=esel[:, :], in_=esel[:, :], compare_op=ALU.is_ge, fill=0.0, base=0,
                                        pattern=[[1, HID]], channel_multiplier=-EH))
                link(pool.affine_select(out=esel[:, :], in_=esel[:, :], compare_op=ALU.is_ge, fill=0.0, base=EH - 1,
                                        pattern=[[-1, HID]], channel_multiplier=EH))
                link(pool.iota(rank_i[:, :, :], pattern=[[0, TU], [-1, NE]], base=NE, channel_multiplier=0))
                pool.tensor_copy(rank[:, :, :], rank_i[:, :, :]).then_inc(s_consts, 1)

            def rstd_of(st):
                n = norm_no(st)
                pool.wait_ge(s_var, n + 1)
                pool.tensor_tensor(rstd[:, :], veps[:, :], mhalf[:, :], ALU.pow).then_inc(s_rstd, 1)

            def run(st):
                name, u = st[0], st[1]
                if name in ("norm1", "out"):
                    rstd_of(st)
                if name == "norm1" and u == (0, 0):
                    rest_of_consts()
                if name in ("q1", "k1"):
                    i, n = (0, 1)[name == "k1"], prep_no[u]
                    for j in range(2):
                        wait_read(pool, name, u, j)
                    if n:
                        pool.wait_ge(s_part[i], 3 * n)
                    pool.tensor_tensor(full[i][:, :], rot[i][:, 0], rot[i][:, 1], ALU.add).then_inc(s_full[i], 1)
                if name in ("q2", "k2"):
                    i, n = (0, 1)[name == "k2"], prep_no[u]
                    pool.wait_ge(s_full[i], n + 1)
                    pool.wait_ge(s_part[i], 3 * n + 1)
                    pool.tensor_tensor(rot[i][:, 0], full[i][:, :], part[i][:, 0], ALU.subtract).then_inc(s_rem[i], 1)
                if name in ("q3", "k3"):
                    i, n = (0, 1)[name == "k3"], prep_no[u]
                    pool.wait_ge(s_rem[i], n + 1)
                    pool.wait_ge(s_part[i], 3 * n + 2)
                    pool.tensor_tensor(part[i][:, 2], rot[i][:, 0], part[i][:, 1], ALU.subtract).then_inc(s_part[i], 1)
                if name == "max1":
                    s, par = u, u % 2
                    pool.wait_ge(s_negm, s + 1)
                    if s >= 2:
                        pool.wait_ge(s_mrow, s - 1)
                    m = negm[:, par].rearrange("p h r -> p (h r)")
                    link(pool.tensor_copy(negp[:, par, 0], m))
                    link(pool.tensor_tensor(negr[:, :], m, negp[:, par, 0], ALU.subtract))
                    link(pool.tensor_copy(negp[:, par, 1], negr[:, :]))
                    pool.tensor_tensor(negp[:, par, 2], negr[:, :], negp[:, par, 1], ALU.subtract).then_inc(s_negp, 1)
                if name == "gates":
                    wait_read(pool, "mod", 0, 1)
                    pool.wait_ge(s_ldrest, 80)
                    for b in range(B):
                        pool.tensor_tensor(wog[:, b], wo_sb[:, :], gate[:, b, 0], ALU.mult)
                        pool.tensor_tensor(bog[:, b], bo_sb[:, :], gate[:, b, 0], ALU.mult)
                        last = pool.tensor_tensor(wpg[:, b], wpj_sb[:, :, :],
                                                  gate[:, b, 1:2].to_broadcast([P, 4, D]), ALU.mult)
                    last.then_inc(s_gated, 1)
                if name == "xb":
                    n, w = unit_no[u], 2 * u[0] + u[1]
                    pool.wait_ge(s_gated, 1)
                    pool.wait_ge(s_xn, 1 + norm_no(("norm1", u)))
                    pool.tensor_tensor(xs[:, w], xs[:, w], bog[:, u[0]:u[0] + 1].to_broadcast([P, TU, D]),
                                       ALU.add).then_inc(s_xb, 1)
                if name[0] == "f":
                    c, n = int(name[1]), 4 * unit_no[u] + int(name[1])
                    pool.wait_ge(s_fl, n + 1)
                    if c == 0 and n:
                        wait_read(pool, "y", UNITS[n // 4 - 1])
                    pool.tensor_tensor(fg[:, c], fl[:, :], fl[:, :], ALU.mult).then_inc(s_fg, 1)

            def zero_future(s, gi, grp):
                kt, khalf, c0, banks = grp
                if khalf != STEPS[s][1] or (STEPS[s][1] and gi < TU):
                    return
                G = group_no[(s, gi)]
                last_bank = max(bank_no[i] for i in b_at if b_at[i][0:2] == (s, gi))
                pool.wait_ge(s_exp, last_bank + 1)
                d = pt[:, G % NP, :, 0:P]
                pool.affine_select(out=d, in_=d, compare_op=ALU.is_ge, fill=0.0, base=0,
                                   pattern=[[0, HG], [1, P]], channel_multiplier=-1).then_inc(s_tri, 1)

            for st in PRE:
                run(st)
            for i in range(slots):
                if i in b_at and b_at[i][4]:
                    zero_future(*b_at[i][0:3])
                for st in stages.get(i, []):
                    run(st)

        @block.scalar
        def _(act):
            act.wait_ge(s_ldmod, 32)
            act.activation(sig[:, 0], ct_sb[:, :], ACT.Exp, scale=-1.0).then_inc(s_exp0, 1)

            def affine(st, dst, which):
                b = st[1][0]
                src, free = side_ready(act, st)
                wait_read(act, "mod", 0)
                act.activation(dst, src, ACT.Identity, bias=modcol[:, which, b:b + 1],
                               scale=modcol[:, which + 1, b:b + 1]).then_inc(free, 1)

            def run(st):
                name, u = st[0], st[1]
                if name == "hT":
                    if prep_no[u]:
                        wait_read(act, "v", PREPS[prep_no[u] - 1])
                    affine(st, ht[:, :], 0)
                if name in ("q2", "k2"):
                    i, n = (0, 1)[name == "k2"], prep_no[u]
                    act.wait_ge(s_full[i], n + 1)
                    if n:
                        act.wait_ge(s_store[i], (5, 3)[i] * 16 * n)
                    act.activation(part[i][:, 0], full[i][:, :], ACT.Copy).then_inc(s_part[i], 1)
                if name in ("q3", "k3"):
                    i, n = (0, 1)[name == "k3"], prep_no[u]
                    act.wait_ge(s_rem[i], n + 1)
                    act.activation(part[i][:, 1], rot[i][:, 0], ACT.Copy).then_inc(s_part[i], 1)
                if name == "max2":
                    s = u
                    act.wait_ge(s_mrow, s + 1)
                    if s >= 2:
                        act.wait_ge(s_mstack[s % 2], 48 * (s // 2))
                    src = ps_m[0:PARTS * HG * TU, 0, 0:P // 2].bitcast(BF16)
                    act.activation(negt[:, s % 2, :], src, ACT.Copy).then_inc(s_negt, 1)
                if name == "o":
                    s = u
                    act.wait_ge(s_pv, group_no[(s, len(groups_b(STEPS[s][1])) - 1)] + 1)
                    if s >= NG:
                        wait_read(act, f"n{TU - 1}", UNITS[s // NG - 1])
                    act.activation(ot[:, s % NG, :], ps_o[:, 0, :], ACT.Copy).then_inc(s_ot, 1)
                if name == "oT":
                    src, free = side_ready(act, st)
                    act.activation(ont[:, :], src, ACT.Copy).then_inc(free, 1)
                if name == "h2":
                    affine(st, h2t[:, :], 2)
                if name == "ohT":
                    src, free = side_ready(act, st)
                    act.activation(oht[:, :], src[0:NE, :], ACT.Copy).then_inc(free, 1)
                if name[0] == "f":
                    n = 4 * unit_no[u] + int(name[1])
                    src, free = side_ready(act, st)
                    if n:
                        wait_read(act, f"f{(n - 1) % 4}", UNITS[(n - 1) // 4], 1)
                    act.activation(fa[:, :], src, ACT.Copy).then_inc(free, 1)

            def exp(i):
                s, gi, grp, (h0, nh), _ = b_at[i]
                n, G, c0 = bank_no[i], group_no[(s, gi)], grp[2]
                act.wait_ge(s_b, n + 1)
                if G >= NP:
                    act.wait_ge(s_pv, G - NP + 1)
                w = HALF - c0
                src = ps_b[:, n % 2, 0:nh * w].rearrange("p (h q) -> p h q", h=nh)
                act.activation(pt[:, G % NP, h0:h0 + nh, 0:w], src, ACT.Exp, scale=SCALE).then_inc(s_exp, 1)

            for st in PRE:
                run(st)
            for i in range(slots):
                if i in b_at:
                    exp(i)
                for st in stages.get(i, []):
                    run(st)

        @block.vector
        def _(dve):
            count = [0]

            def link(ins):
                count[0] += 1
                ins.then_inc(s_dve, 1)
                dve.wait_ge(s_dve, count[0])

            def modulation():
                dve.wait_ge(s_exp0, 1)
                link(dve.tensor_scalar(sig[:, 1], sig[:, 0], 1.0, None, ALU.add))
                link(dve.reciprocal(sig[:, 2], sig[:, 1]))
                link(dve.tensor_tensor(silu[:, :], ct_sb[:, :], sig[:, 2], ALU.mult))
                for b in range(B):
                    last = dve.tensor_copy(silu_b[:, b], silu[:, b:b + 1].to_broadcast([P, P]))
                last.then_inc(s_silu, 1)
                st = ("mod", 0)
                src, free = side_ready(dve, st, 0)
                cols = src[:, 0:4 * B].rearrange("p (j b) -> p j b", b=B)
                link(dve.tensor_copy(modcol[:, 0:4:2], cols[:, 0:4:2]))
                dve.tensor_scalar(modcol[:, 1:4:2], cols[:, 1:4:2], 1.0, None, ALU.add).then_inc(free, 1)
                src, free = side_ready(dve, st, 1)
                g2 = gate[:, :, :, :].rearrange("p b j d -> p (b j d)")
                link(dve.tensor_scalar(gneg[:, :], src, -1.0, None, ALU.mult))
                link(dve.scalar_tensor_tensor(out=gneg[:, :], in0=gneg[:, :], scalar=0.25, in1=src,
                                              op0=ALU.max, op1=ALU.max))
                link(dve.tensor_scalar(g2, src, 0.0, 2.0, ALU.is_ge, ALU.mult))
                dve.scalar_tensor_tensor(out=g2, in0=g2, scalar=-1.0, in1=gneg[:, :],
                                         op0=ALU.add, op1=ALU.mult).then_inc(free, 1)

            def statistics(src, n):
                if n:
                    dve.wait_ge(s_xn, n)
                for t in range(TU):
                    last = dve.bn_stats(stats[:, t], src[:, t])
                link(last)
                for t in range(TU):
                    last = dve.bn_aggr(mv[:, t], stats[:, t])
                link(last)
                dve.tensor_scalar(veps[:, :], mv[:, :, 1], EPS, None, ALU.add).then_inc(s_var, 1)

            def normalise(dst, src, n):
                dve.wait_ge(s_rstd, n + 1)
                for t in range(TU):
                    last = dve.tensor_scalar(dst[:, t], src[:, t], mv[:, t, 0:1], rstd[:, t:t + 1],
                                             ALU.subtract, ALU.mult)
                last.then_inc(s_xn, 1)

            def run(st):
                name, u = st[0], st[1]
                if name == "mod":
                    modulation()
                if name == "norm1":
                    w = 2 * u[0] + u[1]
                    dve.wait_ge(s_ldx[w], 16)
                    statistics(xs[:, w], norm_no(st))
                    if prep_no[u]:
                        wait_read(dve, "hT", PREPS[prep_no[u] - 1])
                    normalise(xn, xs[:, w], norm_no(st))
                if name in ("q1", "k1"):
                    i = (0, 1)[name == "k1"]
                    if name == "q1" and prep_no[u] == 0:
                        dve.wait_ge(s_ldqkv, 80)
                    if prep_no[u]:
                        dve.wait_ge(s_part[i], 3 * prep_no[u])
                    for j in range(2):
                        src, free = side_ready(dve, st, j)
                        dve.scalar_tensor_tensor(out=rot[i][:, j], in0=src, scalar=bcol_sb[:, 2 * i + j:2 * i + j + 1],
                                                 in1=rope_sb[:, j, HALF * u[1]:HALF * u[1] + HALF],
                                                 op0=ALU.add, op1=ALU.mult).then_inc(free, 1)
                if name == "v":
                    w = TU * (2 * u[0] + u[1])
                    src, free = side_ready(dve, st)
                    dve.wait_ge(s_consts, 1)
                    for t in range(TU):
                        last = dve.tensor_tensor(
                            v_sb[:, w + t, 0:H * VW].rearrange("p (h c) -> p h c", c=VW)[:, :, 0:HD],
                            src[:, t * D:t * D + D].rearrange("p (h d) -> p h d", d=HD),
                            bv_sb[:, :].rearrange("p (h d) -> p h d", d=HD), ALU.add)
                    last.then_inc(free, 1)
                if name == "max1":
                    s, half = u, STEPS[u][1]
                    dve.wait_ge(s_max, a_end[s])
                    if s >= 2:
                        dve.wait_ge(s_negp, s - 1)
                    n = 3 if half else 2
                    dve.tensor_reduce(negm[:, s % 2].rearrange("p h r -> p r h"),
                                      tmax[half][:, s % 2, 0:n].rearrange("p k r h -> p r h k"), AX.X, ALU.max,
                                      negate=True).then_inc(s_negm, 1)
                if name[0] == "n" and name != "norm1":
                    t, n = int(name[1]), TU * unit_no[u] + int(name[1])
                    src, free = side_ready(dve, st)
                    heads = src.rearrange("p (g h c) -> p g h c", g=NG, c=32)
                    if n:
                        wait_read(dve, f"n{(n - 1) % TU}", UNITS[(n - 1) // TU])
                    link(dve.reciprocal(rden[:, :, :], heads[:, :, :, HD]))
                    if t == 0 and n:
                        wait_read(dve, "oT", UNITS[n // TU - 1])
                    dve.tensor_tensor(on[:, t].rearrange("p (g h d) -> p g h d", g=NG, d=HD), heads[:, :, :, 0:HD],
                                      rden[:, :, :].unsqueeze(3).to_broadcast([P, NG, HG, HD]),
                                      ALU.mult).then_inc(free, 1)
                if name == "out":
                    n, w = unit_no[u], 2 * u[0] + u[1]
                    src, free = side_ready(dve, st)
                    dve.wait_ge(s_xb, n + 1)
                    dve.tensor_tensor(x2[:, :, :], src.rearrange("p (t d) -> p t d", d=D), xs[:, w],
                                      ALU.add).then_inc(free, 1)
                    wait_read(dve, "out", u)
                    statistics(x2, norm_no(st))
                if name == "ln":
                    normalise(xn2, x2, norm_no(("out", u)))
                if name == "rt":
                    n = unit_no[u]
                    src, free = side_ready(dve, st)
                    lg = src[:, 0:TU * NE].rearrange("p (t e) -> p t e", e=NE)
                    dve.wait_ge(s_consts, 1)
                    link(dve.tensor_reduce(lmax[:, :], lg, AX.X, ALU.max))
                    link(dve.tensor_tensor(leq[:, :, :], lg, lmax[:, :].unsqueeze(2).to_broadcast([P, TU, NE]),
                                           ALU.is_equal))
                    link(dve.tensor_tensor(leq[:, :, :], leq[:, :, :], rank[:, :, :], ALU.mult))
                    link(dve.tensor_reduce(lmax[:, :], leq[:, :, :], AX.X, ALU.max))
                    dve.tensor_tensor(onehot[:, :, :], leq[:, :, :], lmax[:, :].unsqueeze(2).to_broadcast([P, TU, NE]),
                                      ALU.is_equal).then_inc(free, 1)
                if name[0] == "f":
                    n = 4 * unit_no[u] + int(name[1])
                    wait_read(dve, name, u, 0)
                    src, free = side_ready(dve, st, 1)
                    if n:
                        dve.wait_ge(s_fg, n)
                    dve.tensor_tensor(fm[:, :], src, fa[:, :], ALU.mult).then_inc(free, 1)
                    wait_read(dve, name, u, 1)
                    dve.scalar_tensor_tensor(out=fl[:, :], in0=fm[:, :], scalar=0.5, in1=fm[:, :],
                                             op0=ALU.mult, op1=ALU.max).then_inc(s_fl, 1)
                if name == "y":
                    n = unit_no[u]
                    src, free = side_ready(dve, st)
                    if n:
                        dve.wait_ge(s_out, 16 * n)
                    dve.tensor_tensor(y[:, :, :], src.rearrange("p (t d) -> p t d", d=D), x2[:, :, :],
                                      ALU.add).then_inc(free, 1)

            for half in range(2):
                last = dve.memset(tmax[half][:, :, 1], LOW)
            link(last)
            for st in PRE:
                run(st)
            for i in range(slots):
                if i in a_at:
                    s, (kind, r, h0, nh, nk) = a_at[i]
                    dve.wait_ge(s_a, i + 1)
                    src = ps_a[:, i % 2, 0:nh * nk].rearrange("p (h k) -> p h k", h=nh)
                    if s >= 2 and a_at[i - 1][0] != s:
                        dve.wait_ge(s_negm, s - 1)
                    dst = tmax[STEPS[s][1]][:, s % 2, ("diag", "tri", "sq").index(kind), r, h0:h0 + nh]
                    dve.tensor_reduce(dst, src, AX.X, ALU.max).then_inc(s_max, 1)
                for st in stages.get(i, []):
                    run(st)

        @block.tensor
        def _(pe):
            def fill(st, k=0):
                ap, i, use = side(st, k)
                if use:
                    pe.wait_ge(s_sfree[i], use)
                return ap, s_side[i]

            def run(st):
                name, u = st[0], st[1]
                if name == "mod":
                    pe.wait_ge(s_ldmod, 32)
                    pe.wait_ge(s_silu, 1)
                    dst, full_ = fill(st, 0)
                    for j, k in enumerate([0, 1, 3, 4]):
                        last = pe.matmul(dst[:, B * j:B * j + B], wmod_sb[:, D * k:D * k + D], silu[:, :],
                                         start=True, stop=True)
                    last.then_inc(full_, 1)
                    dst, full_ = fill(st, 1)
                    for b in range(B):
                        for j, k in enumerate([2, 5]):
                            c = (2 * b + j) * D
                            last = pe.matmul(dst[:, c:c + D], silu_b[:, b], wmod_sb[:, D * k:D * k + D],
                                             start=True, stop=True)
                    last.then_inc(full_, 1)
                if name in ("hT", "h2"):
                    src = xn if name == "hT" else xn2
                    pe.wait_ge(s_ident, 1)
                    pe.wait_ge(s_xn, 1 + norm_no(("norm1", u) if name == "hT" else ("out", u)))
                    dst, full_ = fill(st)
                    for t in range(TU):
                        last = pe.transpose(dst[:, P * t:P * t + P], src[:, t], ident[:, :])
                    last.then_inc(full_, 1)
                if name in ("q1", "k1"):
                    i = (0, 1)[name == "k1"]
                    if i == 0:
                        pe.wait_ge(s_ldqkv, 80)
                    wait_read(pe, "hT", u)
                    for j, w in enumerate((wqkv_sb, wsw_sb)):
                        dst, full_ = fill(st, j)
                        pe.matmul(dst, w[:, D * i:D * i + D], ht[:, :], start=True, stop=True).then_inc(full_, 1)
                if name == "v":
                    dst, full_ = fill(st)
                    for t in range(TU):
                        last = pe.matmul(dst[:, D * t:D * t + D], ht[:, P * t:P * t + P], wqkv_sb[:, 2 * D:3 * D],
                                         start=True, stop=True)
                    last.then_inc(full_, 1)
                if name == "max2":
                    s = u
                    pe.wait_ge(s_negp, s + 1)
                    if s:
                        pe.wait_ge(s_negt, s)
                    pe.transpose(ps_m[0:PARTS * HG * TU, 0, 0:P // 2].bitcast(BF16),
                                 negp[:, s % 2].rearrange("p c m -> p (c m)"), identb[:, :]).then_inc(s_mrow, 1)
                if name[0] == "n" and name != "norm1":
                    t = int(name[1])
                    pe.wait_ge(s_ot, NG * (unit_no[u] + 1))
                    dst, full_ = fill(st)
                    for g in range(NG):
                        last = pe.transpose(dst[:, P * g:P * g + P], ot[:, g, P * t:P * t + P], ident[:, :])
                    last.then_inc(full_, 1)
                if name == "oT":
                    for t in range(TU):
                        wait_read(pe, f"n{t}", u)
                    dst, full_ = fill(st)
                    for t in range(TU):
                        last = pe.transpose(dst[:, P * t:P * t + P], on[:, t], ident[:, :])
                    last.then_inc(full_, 1)
                if name == "out":
                    wait_read(pe, "oT", u)
                    pe.wait_ge(s_gated, 1)
                    dst, full_ = fill(st)
                    for t in range(TU):
                        last = pe.matmul(dst[:, D * t:D * t + D], ont[:, P * t:P * t + P], wog[:, u[0]],
                                         start=True, stop=True)
                    last.then_inc(full_, 1)
                if name == "rt":
                    wait_read(pe, "h2", u)
                    dst, full_ = fill(st)
                    for t in range(TU):
                        last = pe.matmul(dst[:, NE * t:NE * t + NE], h2t[:, P * t:P * t + P], wr_sb[:, :],
                                         start=True, stop=True)
                    last.then_inc(full_, 1)
                if name == "ohT":
                    wait_read(pe, "rt", u)
                    dst, full_ = fill(st)
                    for t in range(TU):
                        last = pe.transpose(dst[0:NE, P * t:P * t + P], onehot[:, t], ident[:, :])
                    last.then_inc(full_, 1)
                if name[0] == "f":
                    c = int(name[1])
                    dst, full_ = fill(st, 0)
                    pe.matmul(dst, wfc_sb[:, P * c:P * c + P], h2t[:, :], start=True, stop=True).then_inc(full_, 1)
                    if c == 0:
                        wait_read(pe, "ohT", u)
                    dst, full_ = fill(st, 1)
                    pe.matmul(dst, esel[:, P * c:P * c + P], oht[:, :], start=True, stop=True).then_inc(full_, 1)
                if name == "y":
                    pe.wait_ge(s_fg, 4 * (unit_no[u] + 1))
                    dst, full_ = fill(st)
                    for t in range(TU):
                        for c in range(4):
                            last = pe.matmul(dst[:, D * t:D * t + D], fg[:, c, P * t:P * t + P], wpg[:, u[0], c],
                                             start=(c == 0), stop=(c == 3))
                    last.then_inc(full_, 1)

            def stack_ready(s):
                b, half, g = STEPS[s]
                for hf in ((0, 1) if half or b else (0,)):
                    pe.wait_ge(s_stack[hf][g], 6 * 16 * (b + 1))

            def pass_a(i):
                s, (kind, r, h0, nh, nk) = a_at[i]
                b, half, g = STEPS[s]
                if i == 0:
                    pe.wait_ge(s_mask, 1)
                if i == 0 or a_at[i - 1][0] != s:
                    stack_ready(s)
                if i >= 2:
                    pe.wait_ge(s_max, i - 1)
                dst = ps_a[:, i % 2, :]
                if kind == "diag":
                    pe.matmul(dst, identb[:, :], maska[:, :, :].rearrange("p h k -> p (h k)"), start=True, stop=False,
                              skip_group_check=True)
                for j in range(nh):
                    h = HG * g + h0 + j
                    k0, kh = (r * P, half) if kind == "diag" else (0, half) if kind == "tri" else (0, 0)
                    last = pe.matmul(dst[:, j * nk:(j + 1) * nk], qst[0:ROWS, half, h, r * P:r * P + P],
                                     kst[0:ROWS, kh, h, k0:k0 + nk], start=(kind != "diag"), stop=True,
                                     skip_group_check=True)
                last.then_inc(s_a, 1)

            def pass_b(i):
                s, gi, (kt, kh, c0, _), (h0, nh), _ = b_at[i]
                b, half, g = STEPS[s]
                n, w = bank_no[i], HALF - c0
                if gi == 0 and h0 == 0:
                    pe.wait_ge(s_mstack[s % 2], 48 * (s // 2 + 1))
                if n >= 2:
                    pe.wait_ge(s_exp, n - 1)
                for j in range(nh):
                    h = HG * g + h0 + j
                    last = pe.matmul(ps_b[:, n % 2, j * w:(j + 1) * w], kst[:, kh, h, kt * P:kt * P + P],
                                     qst[:, half, h, c0:HALF], start=True, stop=True)
                last.then_inc(s_b, 1)

            def times_v(s, gi, grp):
                kt, kh, c0, banks = grp
                b, half, g = STEPS[s]
                G, n = group_no[(s, gi)], len(groups_b(half))
                pe.wait_ge(s_exp, max(bank_no[i] for i in b_at if b_at[i][0:2] == (s, gi)) + 1)
                diagonal = gi >= n - TU
                if diagonal:
                    pe.wait_ge(s_tri, TU * s + gi - (n - TU) + 1)
                if gi == 0 and s:
                    pe.wait_ge(s_ot, s)
                if gi == 0:
                    wait_read(pe, "v", (b, 1) if half or b else (b, 0))
                for j in range(HG):
                    c = (HG * g + j) * VW
                    last = pe.matmul(ps_o[32 * j:32 * j + 32, 0, c0:HALF], v_sb[:, TU * (2 * b + kh) + kt, c:c + 32],
                                     pt[:, G % NP, j, 0:HALF - c0], start=(gi == 0), stop=(gi == n - 1))
                last.then_inc(s_pv, 1)

            for st in PRE:
                run(st)
            for i in range(slots):
                if i in a_at:
                    pass_a(i)
                if i in b_at:
                    pass_b(i)
                if i in v_at:
                    times_v(*v_at[i])
                for st in stages.get(i, []):
                    run(st)


def rope_tables():
    import numpy as np
    inv = (1.0 / 10000.0 ** (np.arange(0, HD, 2, dtype=np.float32) / np.float32(HD))).astype(np.float32)
    f = np.arange(T, dtype=np.float32)[:, None] * inv[None, :]
    r = np.concatenate([np.sin(f), np.cos(f)], axis=-1).astype(np.float32)
    sin, cos = r[:, ::2], r[:, 1::2]
    c = np.repeat(cos, 2, axis=1)
    s = np.stack([-sin, sin], axis=-1).reshape(T, HD)
    return np.ascontiguousarray(np.stack([np.tile(c.T, (H, 1)), np.tile(s.T, (H, 1))], axis=1))


def kernel(**inputs):
    import numpy as np
    import concourse.bacc as bacc
    from concourse.bass_utils import run_bass_kernel_spmd as run

    a = {k[3:]: np.asarray(v) for k, v in inputs.items()}
    swap = np.arange(2 * D) ^ 1
    qkv_b = a["attn_qkv_b"]
    data = {
        "x": a["attn_x"].reshape(B * 2, TU, P, D).transpose(0, 2, 1, 3),
        "ct": a["c"].T,
        "wmod": a["wmod"],
        "wqkv": a["attn_qkv_w"],
        "wsw": a["attn_qkv_w"][:, swap],
        "bcol": np.stack([qkv_b[:D], qkv_b[swap[:D]], qkv_b[D:2 * D], qkv_b[swap[D:]]], axis=1),
        "bv": qkv_b[2 * D:],
        "wo": a["attn_out_w"],
        "bo": a["attn_out_b"],
        "wr": a["ffn_w_router"].T,
        "wfc": a["ffn_w_fc"].reshape(HID, D).T,
        "wpj": a["ffn_w_proj"].transpose(0, 2, 1).reshape(4, P, D).transpose(1, 0, 2),
        "rope": rope_tables(),
    }
    data = {f"in_{k}": np.ascontiguousarray(v) for k, v in data.items()}
    nc = bacc.Bacc("TRN2", target_bir_lowering=False, num_devices=1)
    args = [nc.dram_tensor(k, v.shape, mybir.dt.from_np(v.dtype), kind="ExternalInput").ap() for k, v in data.items()]
    out = nc.dram_tensor("out", (B * 2, P, TU, D), F32, kind="ExternalOutput").ap()
    adaln_block(nc, *args, out)
    got = run(nc, [data], core_ids=[0]).results[0]["out"]
    return got.transpose(0, 2, 1, 3).reshape(B, T, D)
```

```python
from contextlib import ExitStack

import concourse.bass as bass
from concourse import mybir

ALU = mybir.AluOpType
ACT = mybir.ActivationFunctionType
AX = mybir.AxisListType
F32 = mybir.dt.float32
BF16 = mybir.dt.bfloat16
I32 = mybir.dt.int32

P = 128
B, T, D = 2, 1024, 128
H = 16
HD = D // H
NE, EH = 8, 64
HID = NE * EH
HALF = T // 2
TU = HALF // P
HG = 4
NG = H // HG
PARTS = 3
ROWS = PARTS * PARTS * HD
ROWSM = ROWS + PARTS
VW = HD + 1
VPAD = H * VW + 24
SCALE = float(HD) ** -0.5
EPS = 1e-5
ONES = 1 + 0x3F80 / 2 ** 23
LOW = -(2.0 ** 127)

UNITS = [(0, 0), (0, 1), (1, 1), (1, 0)]
PREPS = [(0, 0), (0, 1), (1, 0), (1, 1)]
PIECES = {u: [(0, TU)] for u in UNITS}
PIECES[UNITS[-1]] = [(0, TU // 2), (TU // 2, TU)]
STEPS = [(b, half, g) for b, half in UNITS for g in range(NG)]


def bank_jobs_a(half):
    jobs = []
    for r in range(TU):
        jobs.append(("diag", r, 0, HG, P))
        if r:
            nh = min(HG, HALF // (r * P)) if r < 3 else 1
            jobs += [("tri", r, h, nh, r * P) for h in range(0, HG, nh)]
        if half:
            jobs += [("sq", r, h, 1, HALF) for h in range(HG)]
    return jobs


def groups_b(half):
    out = []
    if half:
        out += [(kt, 0, 0, [(h, 1) for h in range(HG)]) for kt in range(TU)]
    for kt in range(TU):
        n = HALF - kt * P
        nh = max(1, HALF // n) if n < 384 else 1
        out.append((kt, half, kt * P, [(h, nh) for h in range(0, HG, nh)]))
    return out


LEAD = 8
PVLAG = 3
SIDES = 2

BANKS_OF = {"mod": 1, "gate": 1, "hT": 1, "q1": 2, "k1": 2, "v": 1, "max2": 1, "oT": 1, "out": 1, "h2": 1, "rt": 1,
            "ohT": 1, "y0": 1, "y1": 1, **{f"n{g}": 1 for g in range(NG)}, **{f"a{c}": 1 for c in range(4)},
            **{f"m{c}": 1 for c in range(4)}}
PREP = {"norm1": 0, "nz": 2, "hT": 3, "q1": 3, "q2": 3, "q3": 3, "k1": 3, "k2": 3, "k3": 3, "v": 5}
POST = {"oT": 2, "out": 2, "ln": 3, "h2": 3, "rt": 2, "a0": 2, "a1": 2, "ohT": 2, "a2": 2, "a3": 2, "m0": 2, "m1": 2,
        "m2": 2, "y0": 1, "m3": 3, "y1": 4}
POST_LAST = ["oT", "out", "ln", "h2", "rt", "a0", "a1", "ohT", "m0", "a2", "m1", "a3", "m2", "y0", "m3", "y1"]
PREP_AT = [[0, 0], [40, 1], [86, 1]]
MAX_LAG = 3
O_LAG = 3
GATES_AT = 30

WARM_PRE = {"start": 7, "mod": 8, "hT": 4, "v": 30}
WARM_POST = {"n3": 3, "oT": 1, "out": 7, "h2": 1}
HIDDEN = ("a0", "a1", "a2", "a3")

PRE = [("mod", 0)] + [(name, (0, 0)) for name in ["norm1", "nz", "hT", "q1", "k1", "q2", "q3", "k2", "k3", "v"]] \
    + [("load", (0, 0), g) for g in range(NG)] + [(name, (0, 1)) for name in ["norm1", "nz", "hT"]]


def plan():
    a_at, a_end, n = {}, [], 0
    for s, (b, half, g) in enumerate(STEPS):
        for job in bank_jobs_a(half):
            a_at[n] = (s, job)
            n += 1
        a_end.append(n)
    b_at, v_at, stages = {}, {}, {}
    slot, v_end = 0, []
    for s, (b, half, g) in enumerate(STEPS):
        slot = max(slot, a_end[s] + LEAD)
        for gi, grp in enumerate(groups_b(half)):
            for bank in grp[3]:
                b_at[slot] = (s, gi, grp, bank, bank is grp[3][-1])
                slot += 1
            v_at[slot - 1 + PVLAG] = (s, gi, grp)
        v_end.append(slot - 1 + PVLAG)

    def put(at, *stage):
        while sum(BANKS_OF.get(st[0], 0) for st in stages.get(at, [])) + BANKS_OF.get(stage[0], 0) > SIDES:
            at += 1
        stages.setdefault(at, []).append(stage)
        return at

    for s in range(len(STEPS)):
        put(a_end[s] - 1, "max1", s)
        put(a_end[s] + MAX_LAG, "max2", s)
        put(v_end[s], "o", s)
    put(GATES_AT - 8, "gate", 0)
    put(GATES_AT, "gates", 0)
    done = {}
    for u, (at, more) in zip(PREPS[1:], PREP_AT):
        for name, gap in PREP.items():
            if (name, u) not in PRE:
                done[u] = at = put(at + gap + more, name, u)
    for g in range(NG):
        put(done[(0, 1)] + 1, "load", (0, 1), g)
        for half in range(2):
            put(max(v_end[4 + g], done[(1, 1)]) + 1, "load", (1, half), g)
    for s, (b, half, g) in enumerate(STEPS):
        at = put(v_end[s] + O_LAG, f"n{g}", (b, half))
        if g == 2:
            put(at + 1, "xb", (b, half))
        if g == NG - 1:
            for name in POST if (b, half) != UNITS[-1] else POST_LAST:
                at += POST[name]
                for piece in range(len(PIECES[(b, half)])):
                    at = put(at, name, (b, half, piece))
    slots = max(list(a_at) + list(b_at) + list(v_at) + list(stages)) + 1
    return slots, a_at, b_at, v_at, stages, a_end


def adaln_block(nc, x, ct, wmod, wqkv, wsw, bcol, bv, wo, bo, wr, wfc, wpj, rope, out):
    slots, a_at, b_at, v_at, stages, a_end = plan()
    order = list(PRE) + [st for i in range(slots) for st in stages.get(i, [])]
    side_job, count = {}, {"side": 0, "tail": 0}
    for st in order:
        for k in range(BANKS_OF.get(st[0], 0)):
            ring = "tail" if st[0] in HIDDEN + ("y0", "y1") and st[1][0:2] == UNITS[-1] else "side"
            side_job[(st[0], st[1], k)] = (ring, count[ring])
            count[ring] += 1
    group_no = {}
    for i in sorted(b_at):
        group_no.setdefault(b_at[i][0:2], len(group_no))
    bank_no = {i: n for n, i in enumerate(sorted(b_at))}
    prep_no = {u: n for n, u in enumerate(PREPS)}
    unit_no = {u: n for n, u in enumerate(UNITS)}
    pe_at = {i - 1: sts for i, sts in stages.items()}
    qparts = nc.dram_tensor("qparts", (B * 2, 5, HD, H, HALF), BF16)
    kparts = nc.dram_tensor("kparts", (B * 2, PARTS, HD, H, HALF), BF16)

    with ExitStack() as ctx:
        def sb(name, shape, dt=F32):
            return ctx.enter_context(nc.sbuf_tensor(name, shape, dt))

        def bank(name, n=1):
            return ctx.enter_context(nc.psum_tensor(name, [P, n, HALF], F32))

        def sem(name):
            return ctx.enter_context(nc.semaphore(name))

        ct_sb = sb("ct_sb", [P, B])
        wmod_sb = sb("wmod_sb", [P, 6 * D])
        wqkv_sb = sb("wqkv_sb", [P, 3 * D])
        wsw_sb = sb("wsw_sb", [P, 2 * D])
        bcol_sb = sb("bcol_sb", [P, 4])
        bv_sb = sb("bv_sb", [P, D])
        bo_sb = sb("bo_sb", [P, D])
        wo_sb = sb("wo_sb", [P, D])
        wr_sb = sb("wr_sb", [P, NE])
        wfc_sb = sb("wfc_sb", [P, HID])
        wpj_sb = sb("wpj_sb", [P, 4, D])
        rope_sb = sb("rope_sb", [P, 2, T])
        ident = sb("ident", [P, P])
        identb = sb("identb", [P, P], BF16)
        maska = sb("maska", [P, HG, P], BF16)
        esel = sb("esel", [NE, HID], BF16)
        rank_i = sb("rank_i", [P, TU, NE], I32)
        rank = sb("rank", [P, TU, NE])
        ones = sb("ones", [P, 1])
        mhalf = sb("mhalf", [P, TU])
        sig = sb("sig", [P, 3, B])
        silu = sb("silu", [P, B])
        silu_b = sb("silu_b", [P, B, P])
        modcol = sb("modcol", [P, 4, B])
        gneg = sb("gneg", [P, 2 * B * D])
        gate = sb("gate", [P, B, 2, D])
        wog = sb("wog", [P, B, D])
        bog = sb("bog", [P, B, D])
        wpg = sb("wpg", [P, B, 4, D])
        xs = sb("xs", [P, B * 2, TU, D])
        stats = sb("stats", [P, TU, 6])
        mv = sb("mv", [P, TU, 2])
        veps = sb("veps", [P, TU])
        rstd = sb("rstd", [P, TU])
        xn = sb("xn", [P, TU, D])
        ht = sb("ht", [P, HALF])
        rot = [sb(f"rot{i}", [P, 2, HALF]) for i in range(2)]
        full = [sb(f"full{i}", [P, HALF]) for i in range(2)]
        part = [sb(f"part{i}", [P, PARTS, HALF], BF16) for i in range(2)]
        qst = sb("qst", [ROWSM, 2, H, HALF], BF16)
        kst = sb("kst", [ROWSM, 2, H, HALF], BF16)
        v_sb = sb("v_sb", [P, B * 2 * TU, VPAD])
        tmax = [sb(f"tmax{i}", [P, 2, 3, TU, HG]) for i in range(2)]
        negm = sb("negm", [P, 2, HG, TU])
        negr = sb("negr", [P, HG * TU])
        negp = sb("negp", [P, 2, PARTS, HG * TU], BF16)
        negt = sb("negt", [PARTS * HG * TU, 2, P], BF16)
        NP = 4
        pt = sb("pt", [P, NP, HG, HALF])
        ot = sb("ot", [P, NG, HALF])
        rden = sb("rden", [P, TU, HG])
        on = sb("on", [P, TU, D])
        ont = sb("ont", [P, HALF])
        x2 = sb("x2", [P, TU, D])
        xn2 = sb("xn2", [P, TU, D])
        h2t = sb("h2t", [P, HALF])
        lmax = sb("lmax", [P, TU])
        leq = sb("leq", [P, TU, NE])
        onehot = sb("onehot", [P, TU, NE])
        oht = sb("oht", [NE, HALF], BF16)
        fa = sb("fa", [P, 2, HALF])
        fg = sb("fg", [P, 4, HALF])
        y = sb("y", [P, TU, D])

        NA = 3
        ps_a = bank("ps_a", NA)
        ps_b = bank("ps_b", 2)
        ps_o = bank("ps_o")
        ps_s = bank("ps_s", 2)

        s_ldx = [sem(f"s_ldx{i}") for i in range(B * 2)]
        s_ldct, s_ldmod, s_ldqkv, s_ldbv = sem("s_ldct"), sem("s_ldmod"), sem("s_ldqkv"), sem("s_ldbv")
        s_ldrest = sem("s_ldrest")
        s_ident, s_mask, s_consts = sem("s_ident"), sem("s_mask"), sem("s_consts")
        s_one, s_ones, s_vones = sem("s_one"), sem("s_ones"), sem("s_vones")
        s_pool = sem("s_pool")
        s_dve = sem("s_dve")
        s_exp0, s_silu, s_gated = sem("s_exp0"), sem("s_silu"), sem("s_gated")
        s_var, s_rstd, s_xn = sem("s_var"), sem("s_rstd"), sem("s_xn")
        s_full = [sem(f"s_full{i}") for i in range(2)]
        s_part = [sem(f"s_part{i}") for i in range(2)]
        s_rem = [sem(f"s_rem{i}") for i in range(2)]
        s_store = [sem(f"s_store{i}") for i in range(2)]
        s_stack = [[sem(f"s_stack{h}_{g}") for g in range(NG)] for h in range(2)]
        s_a, s_max = sem("s_a"), sem("s_max")
        s_b, s_exp, s_tri, s_pv = sem("s_b"), sem("s_exp"), sem("s_tri"), sem("s_pv")
        s_negm, s_negp = sem("s_negm"), sem("s_negp")
        s_mstack = [sem(f"s_mstack{i}") for i in range(2)]
        s_ot = sem("s_ot")
        s_side = [sem(f"s_side{i}") for i in range(4)]
        s_sfree = [sem(f"s_sfree{i}") for i in range(4)]
        s_xb, s_fl, s_fs, s_out = sem("s_xb"), sem("s_fl"), sem("s_fs"), sem("s_out")

        squares = []
        block = ctx.enter_context(nc.Block())

        def side(st, k=0):
            ring, j = side_job[(st[0], st[1], k)]
            if ring == "side":
                return ps_s[:, j % 2, :], j % 2, j // 2
            return ps_a[:, 1 + j % 2, :], 2 + j % 2, j // 2

        def side_ready(eng, st, k=0):
            ap, i, use = side(st, k)
            eng.wait_ge(s_side[i], use + 1)
            return ap, s_sfree[i]

        def wait_read(eng, name, u, k=0):
            _, i, use = side((name, u), k)
            eng.wait_ge(s_sfree[i], use + 1)

        def nth(st, *names):
            return len([x for x in order[:order.index(st)] if x[0] in names])

        def tiles(u):
            return PIECES[u[0:2]][u[2]]

        def last_piece(n):
            return UNITS[n] + (len(PIECES[UNITS[n]]) - 1,)

        def split(eng, name, u):
            if name in ("q1", "k1"):
                i, n = (0, 1)[name == "k1"], prep_no[u]
                for j in range(2):
                    wait_read(eng, name, u, j)
                if n:
                    eng.wait_ge(s_part[i], 3 * n)
                eng.tensor_tensor(full[i][:, :], rot[i][:, 0], rot[i][:, 1], ALU.add).then_inc(s_full[i], 1)
            if name in ("q2", "k2"):
                i, n = (0, 1)[name == "k2"], prep_no[u]
                eng.wait_ge(s_full[i], n + 1)
                eng.wait_ge(s_part[i], 3 * n + 1)
                eng.tensor_tensor(rot[i][:, 0], full[i][:, :], part[i][:, 0], ALU.subtract).then_inc(s_rem[i], 1)
            if name in ("q3", "k3"):
                i, n = (0, 1)[name == "k3"], prep_no[u]
                eng.wait_ge(s_rem[i], n + 1)
                eng.wait_ge(s_part[i], 3 * n + 2)
                eng.tensor_tensor(part[i][:, 2], rot[i][:, 0], part[i][:, 1], ALU.subtract).then_inc(s_part[i], 1)

        @block.sync
        def _(sp):
            sp.dma_start(xs[:, 0], x[0]).then_inc(s_ldx[0], 16)
            sp.dma_start(wqkv_sb[:, :], wqkv).then_inc(s_ldqkv, 16)
            sp.dma_start(wsw_sb[:, :], wsw).then_inc(s_ldqkv, 16)
            sp.dma_start(bcol_sb[:, :], bcol).then_inc(s_ldqkv, 16)
            sp.dma_start(rope_sb[:, :, :], rope).then_inc(s_ldqkv, 16)
            sp.dma_start(bv_sb[:, :], bv.partition_broadcast(P)).then_inc(s_ldbv, 16)
            for i in range(1, B * 2):
                sp.dma_start(xs[:, i], x[i]).then_inc(s_ldx[i], 16)
            sp.dma_start(bo_sb[:, :], bo.partition_broadcast(P)).then_inc(s_ldrest, 16)
            sp.dma_start(wo_sb[:, :], wo).then_inc(s_ldrest, 16)
            sp.dma_start(wr_sb[:, :], wr).then_inc(s_ldrest, 16)
            sp.dma_start(wfc_sb[:, :], wfc).then_inc(s_ldrest, 16)
            sp.dma_start(wpj_sb[:, :, :], wpj).then_inc(s_ldrest, 16)

            def store(u, i):
                n, w = prep_no[u], 2 * u[0] + u[1]
                sp.wait_ge(s_part[i], 3 * (n + 1))
                dst = (qparts, kparts)[i].ap()[w].rearrange("j d h t -> (d h) j t")
                sp.dma_start(dst[:, 0:PARTS], part[i][:, :, :]).then_inc(s_store[i], 16)
                if i == 0:
                    sp.dma_start(dst[:, PARTS:5], part[i][:, 0:2, :]).then_inc(s_store[i], 16)

            def load(u, g):
                (b, half), w, n = u, 2 * u[0] + u[1], prep_no[u]
                if b:
                    sp.wait_ge(s_pv, group_no[(NG + g, len(groups_b(1)) - 1)] + 1)
                h0, row, R = HG * g, H * HALF, PARTS * HD
                q = bass.AP(tensor=qparts, offset=w * 5 * HD * row + h0 * HALF,
                            ap=[[HD * row, PARTS], [row, R], [1, HG * HALF]])
                k = bass.AP(tensor=kparts, offset=w * PARTS * HD * row + h0 * HALF,
                            ap=[[0, PARTS], [row, R], [1, HG * HALF]])
                sp.wait_ge(s_ones, half + 1)
                for i, (dst, src) in enumerate(((qst, q), (kst, k))):
                    sp.wait_ge(s_store[i], (2, 1)[i] * 16 * (n + 1))
                    sp.dma_start(dst[0:ROWS, half, h0:h0 + HG, :].rearrange("p h t -> p (h t)"),
                                 src).then_inc(s_stack[half][g], 16)

            def max_rows(s):
                b, half, g = STEPS[s]
                wait_read(sp, "max2", s)
                M = HG * TU
                for p in range(PARTS):
                    dst = qst[ROWS + p:ROWS + p + 1, half, HG * g:HG * g + HG, :].rearrange("o h (r x) -> o (h r) x", x=P)
                    sp.dma_start(dst, negt[M * p:M * p + M, s % 2, :]).then_inc(s_mstack[s % 2], 16)

            def run(st):
                if st[0] in ("q3", "k3"):
                    store(st[1], 0 if st[0] == "q3" else 1)
                if st[0] == "load":
                    load(st[1], st[2])
                if st[0] == "max2":
                    max_rows(st[1])
                if st[0] == "y1":
                    u, (t0, t1) = st[1], tiles(st[1])
                    wait_read(sp, "y1", u)
                    sp.dma_start(out[2 * u[0] + u[1], :, t0:t1], y[:, t0:t1]).then_inc(s_out, 16)

            for st in order:
                run(st)
            sp.wait_ge(s_out, 16 * sum(len(p) for p in PIECES.values()))

        @block.gpsimd
        def _(pool):
            count = [0]

            def link(ins):
                count[0] += 1
                ins.then_inc(s_pool, 1)
                pool.wait_ge(s_pool, count[0])

            link(pool.memset(mhalf[:, :], -0.5))
            link(pool.memset(ident[:, :], 0.0))
            pool.affine_select(out=ident[:, :], in_=ident[:, :], compare_op=ALU.not_equal, fill=1.0, base=0,
                               pattern=[[-1, P]], channel_multiplier=1).then_inc(s_ident, 1)

            pool.wait_ge(s_ident, 1)
            pool.tensor_copy(identb[:, :], ident[:, :])
            link(pool.memset(maska[:, :, :], 0.0))
            pool.affine_select(out=maska[:, :, :], in_=maska[:, :, :], compare_op=ALU.is_ge, fill=LOW, base=0,
                               pattern=[[0, HG], [-1, P]], channel_multiplier=1).then_inc(s_mask, 1)
            pool.memset(v_sb[:, :, H * VW:VPAD], 0.0)
            pool.memset(v_sb[:, :, 0:H * VW].rearrange("p t (h c) -> p t h c", c=VW)[:, :, :, HD],
                        1.0).then_inc(s_vones, 1)

            def router_consts():
                link(pool.memset(esel[:, :], 1.0))
                link(pool.affine_select(out=esel[:, :], in_=esel[:, :], compare_op=ALU.is_ge, fill=0.0, base=0,
                                        pattern=[[1, HID]], channel_multiplier=-EH))
                link(pool.affine_select(out=esel[:, :], in_=esel[:, :], compare_op=ALU.is_ge, fill=0.0, base=EH - 1,
                                        pattern=[[-1, HID]], channel_multiplier=EH))
                link(pool.iota(rank_i[:, :, :], pattern=[[0, TU], [-1, NE]], base=NE, channel_multiplier=0))
                pool.tensor_copy(rank[:, :, :], rank_i[:, :, :]).then_inc(s_consts, 1)

            def rstd_of(st):
                t0, t1 = (0, TU) if st[0] == "norm1" else tiles(st[1])
                pool.wait_ge(s_var, nth(st, "norm1", "out") + 1)
                pool.tensor_tensor(rstd[:, t0:t1], veps[:, t0:t1], mhalf[:, t0:t1], ALU.pow).then_inc(s_rstd, 1)

            def run(st):
                name, u = st[0], st[1]
                if name in ("norm1", "out"):
                    rstd_of(st)
                if name == "gate":
                    router_consts()
                if name in ("q1", "q2", "q3") or name in ("k1", "k2", "k3") and prep_no[u]:
                    split(pool, name, u)
                if name == "max1":
                    s, par = u, u % 2
                    pool.wait_ge(s_negm, s + 1)
                    if s >= 2:
                        wait_read(pool, "max2", s - 2)
                    m = negm[:, par].rearrange("p h r -> p (h r)")
                    link(pool.tensor_copy(negp[:, par, 0], m))
                    link(pool.tensor_tensor(negr[:, :], m, negp[:, par, 0], ALU.subtract))
                    link(pool.tensor_copy(negp[:, par, 1], negr[:, :]))
                    pool.tensor_tensor(negp[:, par, 2], negr[:, :], negp[:, par, 1], ALU.subtract).then_inc(s_negp, 1)
                if name == "gates":
                    wait_read(pool, "gate", 0)
                    pool.wait_ge(s_ldrest, 80)
                    for b in range(B):
                        pool.tensor_tensor(wog[:, b], wo_sb[:, :], gate[:, b, 0], ALU.mult)
                        pool.tensor_tensor(bog[:, b], bo_sb[:, :], gate[:, b, 0], ALU.mult)
                        last = pool.tensor_tensor(wpg[:, b], wpj_sb[:, :, :],
                                                  gate[:, b, 1:2].to_broadcast([P, 4, D]), ALU.mult)
                    last.then_inc(s_gated, 1)
                if name == "xb":
                    n, w = unit_no[u], 2 * u[0] + u[1]
                    pool.wait_ge(s_gated, 1)
                    pool.wait_ge(s_xn, 1 + nth(("nz", u), "nz", "ln"))
                    pool.tensor_tensor(xs[:, w], xs[:, w], bog[:, u[0]:u[0] + 1].to_broadcast([P, TU, D]),
                                       ALU.add).then_inc(s_xb, 1)

            def zero_future(s, gi, grp):
                kt, khalf, c0, banks = grp
                if khalf != STEPS[s][1] or (STEPS[s][1] and gi < TU):
                    return
                G = group_no[(s, gi)]
                last_bank = max(bank_no[i] for i in b_at if b_at[i][0:2] == (s, gi))
                pool.wait_ge(s_exp, last_bank + 1)
                d = pt[:, G % NP, :, 0:P]
                pool.affine_select(out=d, in_=d, compare_op=ALU.is_ge, fill=0.0, base=0,
                                   pattern=[[0, HG], [1, P]], channel_multiplier=-1).then_inc(s_tri, 1)

            for st in PRE:
                run(st)
            for i in range(slots):
                if i in b_at and b_at[i][4]:
                    zero_future(*b_at[i][0:3])
                for st in stages.get(i, []):
                    run(st)

        @block.scalar
        def _(act):
            act.dma_start(ct_sb[:, :], ct).then_inc(s_ldct, 16)
            act.dma_start(wmod_sb[:, :], wmod).then_inc(s_ldmod, 16)
            act.wait_ge(s_ldct, 16)
            act.activation(sig[:, 0], ct_sb[:, :], ACT.Exp, scale=-1.0).then_inc(s_exp0, 1)

            def rows_of_ones(half):
                rows = kst[64:ROWSM, half].rearrange("p h t -> p (h t)").bitcast(F32)
                act.activation(rows, ones[64:ROWSM].to_broadcast([ROWSM - 64, H * HALF // 2]),
                               ACT.Copy).then_inc(s_ones, 1)

            act.wait_ge(s_one, 1)
            rows_of_ones(0)

            def affine(st, dst, which, cols=slice(0, HALF)):
                b = st[1][0]
                src, free = side_ready(act, st)
                wait_read(act, "mod", 0)
                act.activation(dst, src[:, cols], ACT.Identity, bias=modcol[:, which, b:b + 1],
                               scale=modcol[:, which + 1, b:b + 1]).then_inc(free, 1)

            def run(st):
                name, u = st[0], st[1]
                if name == "hT":
                    if prep_no[u]:
                        wait_read(act, "v", PREPS[prep_no[u] - 1])
                    affine(st, ht[:, :], 0)
                if name in ("q2", "k2"):
                    i, n = (0, 1)[name == "k2"], prep_no[u]
                    act.wait_ge(s_full[i], n + 1)
                    if n:
                        act.wait_ge(s_store[i], (2, 1)[i] * 16 * n)
                    act.activation(part[i][:, 0], full[i][:, :], ACT.Copy).then_inc(s_part[i], 1)
                if name in ("q3", "k3"):
                    i, n = (0, 1)[name == "k3"], prep_no[u]
                    act.wait_ge(s_rem[i], n + 1)
                    act.activation(part[i][:, 1], rot[i][:, 0], ACT.Copy).then_inc(s_part[i], 1)
                    if st == ("k3", (0, 0)):
                        rows_of_ones(1)
                if name == "max2":
                    s = u
                    src, free = side_ready(act, st)
                    if s >= 2:
                        act.wait_ge(s_mstack[s % 2], 48 * (s // 2))
                    act.activation(negt[:, s % 2, :], src[0:PARTS * HG * TU, 0:P // 2].bitcast(BF16),
                                   ACT.Copy).then_inc(free, 1)
                if name == "o":
                    s = u
                    act.wait_ge(s_pv, group_no[(s, len(groups_b(STEPS[s][1])) - 1)] + 1)
                    if s >= NG:
                        wait_read(act, f"n{s % NG}", UNITS[s // NG - 1])
                    act.activation(ot[:, s % NG, :], ps_o[:, 0, :], ACT.Copy).then_inc(s_ot, 1)
                if name in POST:
                    t0, t1 = tiles(u)
                    cols = slice(P * t0, P * t1)
                if name == "oT":
                    src, free = side_ready(act, st)
                    act.activation(ont[:, cols], src[:, cols], ACT.Copy).then_inc(free, 1)
                if name == "h2":
                    affine(st, h2t[:, cols], 2, cols)
                if name == "ohT":
                    src, free = side_ready(act, st)
                    act.activation(oht[:, cols], src[0:NE, cols], ACT.Copy).then_inc(free, 1)
                if name[0] == "a":
                    c, n = int(name[1]), nth(st, *HIDDEN)
                    src, free = side_ready(act, st)
                    if n >= 2:
                        act.wait_ge(s_fl, n - 1)
                    act.activation(fa[:, n % 2, cols], src[:, cols], ACT.Copy).then_inc(free, 1)
                    if c:
                        square(u, c - 1)
                    if c == 3:
                        square(u, c)

            def square(u, c):
                t0, t1 = tiles(u)
                cols = slice(P * t0, P * t1)
                act.wait_ge(s_fl, nth((f"a{c}", u), *HIDDEN) + 1)
                squares.append((u, c))
                act.activation(fg[:, c, cols], fg[:, c, cols], ACT.Square).then_inc(s_fs, 1)

            def exp(i):
                s, gi, grp, (h0, nh), _ = b_at[i]
                n, G, c0 = bank_no[i], group_no[(s, gi)], grp[2]
                act.wait_ge(s_b, n + 1)
                if G >= NP:
                    act.wait_ge(s_pv, G - NP + 1)
                w = HALF - c0
                src = ps_b[:, n % 2, 0:nh * w].rearrange("p (h q) -> p h q", h=nh)
                act.activation(pt[:, G % NP, h0:h0 + nh, 0:w], src, ACT.Exp, scale=SCALE).then_inc(s_exp, 1)

            for st in PRE:
                run(st)
            for i in range(slots):
                if i in b_at:
                    exp(i)
                for st in stages.get(i, []):
                    run(st)

        @block.vector
        def _(dve):
            count = [0]

            def link(ins):
                count[0] += 1
                ins.then_inc(s_dve, 1)
                dve.wait_ge(s_dve, count[0])

            def modulation():
                dve.wait_ge(s_exp0, 1)
                link(dve.tensor_scalar(sig[:, 1], sig[:, 0], 1.0, None, ALU.add))
                link(dve.reciprocal(sig[:, 2], sig[:, 1]))
                link(dve.tensor_tensor(silu[:, :], ct_sb[:, :], sig[:, 2], ALU.mult))
                for b in range(B):
                    last = dve.tensor_copy(silu_b[:, b], silu[:, b:b + 1].to_broadcast([P, P]))
                last.then_inc(s_silu, 1)

            def modulation_columns():
                src, free = side_ready(dve, ("mod", 0))
                cols = src[:, 0:4 * B].rearrange("p (j b) -> p j b", b=B)
                link(dve.tensor_copy(modcol[:, 0:4:2], cols[:, 0:4:2]))
                dve.tensor_scalar(modcol[:, 1:4:2], cols[:, 1:4:2], 1.0, None, ALU.add).then_inc(free, 1)

            def gates():
                src, free = side_ready(dve, ("gate", 0))
                g2 = gate[:, :, :, :].rearrange("p b j d -> p (b j d)")
                link(dve.tensor_scalar(gneg[:, :], src, -1.0, None, ALU.mult))
                link(dve.scalar_tensor_tensor(out=gneg[:, :], in0=gneg[:, :], scalar=0.25, in1=src,
                                              op0=ALU.max, op1=ALU.max))
                link(dve.tensor_scalar(g2, src, 0.0, 2.0, ALU.is_ge, ALU.mult))
                dve.scalar_tensor_tensor(out=g2, in0=g2, scalar=-1.0, in1=gneg[:, :],
                                         op0=ALU.add, op1=ALU.mult).then_inc(free, 1)

            def statistics(src, n, t0=0, t1=TU):
                if n:
                    dve.wait_ge(s_xn, n)
                for t in range(t0, t1):
                    last = dve.bn_stats(stats[:, t], src[:, t])
                link(last)
                for t in range(t0, t1):
                    last = dve.bn_aggr(mv[:, t], stats[:, t])
                link(last)
                dve.tensor_scalar(veps[:, t0:t1], mv[:, t0:t1, 1], EPS, None, ALU.add).then_inc(s_var, 1)

            def normalise(dst, src, n, t0=0, t1=TU):
                dve.wait_ge(s_rstd, n + 1)
                for t in range(t0, t1):
                    last = dve.tensor_scalar(dst[:, t], src[:, t], mv[:, t, 0:1], rstd[:, t:t + 1],
                                             ALU.subtract, ALU.mult)
                last.then_inc(s_xn, 1)

            def run(st):
                name, u = st[0], st[1]
                if name == "mod":
                    modulation()
                if name == "norm1":
                    w = 2 * u[0] + u[1]
                    dve.wait_ge(s_ldx[w], 16)
                    statistics(xs[:, w], nth(st, "nz", "ln"))
                if name == "gate":
                    gates()
                if name == "nz":
                    w = 2 * u[0] + u[1]
                    if prep_no[u]:
                        wait_read(dve, "hT", PREPS[prep_no[u] - 1])
                    else:
                        modulation_columns()
                    normalise(xn, xs[:, w], nth(("norm1", u), "norm1", "out"))
                if name in ("q1", "k1"):
                    i = (0, 1)[name == "k1"]
                    if name == "q1" and prep_no[u] == 0:
                        dve.wait_ge(s_ldqkv, 64)
                    if prep_no[u]:
                        dve.wait_ge(s_part[i], 3 * prep_no[u])
                    for j in range(2):
                        src, free = side_ready(dve, st, j)
                        dve.scalar_tensor_tensor(out=rot[i][:, j], in0=src, scalar=bcol_sb[:, 2 * i + j:2 * i + j + 1],
                                                 in1=rope_sb[:, j, HALF * u[1]:HALF * u[1] + HALF],
                                                 op0=ALU.add, op1=ALU.mult).then_inc(free, 1)
                if name in ("k1", "k2", "k3") and prep_no[u] == 0:
                    split(dve, name, u)
                if name == "v":
                    w = TU * (2 * u[0] + u[1])
                    src, free = side_ready(dve, st)
                    dve.wait_ge(s_ldbv, 16)
                    for t in range(TU):
                        last = dve.tensor_tensor(
                            v_sb[:, w + t, 0:H * VW].rearrange("p (h c) -> p h c", c=VW)[:, :, 0:HD],
                            src[:, t * D:t * D + D].rearrange("p (h d) -> p h d", d=HD),
                            bv_sb[:, :].rearrange("p (h d) -> p h d", d=HD), ALU.add)
                    last.then_inc(free, 1)
                if name == "max1":
                    s, half = u, STEPS[u][1]
                    dve.wait_ge(s_max, a_end[s])
                    if s >= 2:
                        dve.wait_ge(s_negp, s - 1)
                    n = 3 if half else 2
                    dve.tensor_reduce(negm[:, s % 2].rearrange("p h r -> p r h"),
                                      tmax[half][:, s % 2, 0:n].rearrange("p k r h -> p r h k"), AX.X, ALU.max,
                                      negate=True).then_inc(s_negm, 1)
                if name[0] == "n" and name[1:].isdigit():
                    g, n = int(name[1]), NG * unit_no[u] + int(name[1])
                    src, free = side_ready(dve, st)
                    heads = src.rearrange("p (t h c) -> p t h c", t=TU, c=32)
                    if n:
                        wait_read(dve, f"n{(n - 1) % NG}", UNITS[(n - 1) // NG])
                    link(dve.reciprocal(rden[:, :, :], heads[:, :, :, HD]))
                    if g == 0 and n:
                        wait_read(dve, "oT", last_piece(n // NG - 1))
                    dve.tensor_tensor(on[:, :, D // NG * g:D // NG * (g + 1)].rearrange("p t (h d) -> p t h d", d=HD),
                                      heads[:, :, :, 0:HD],
                                      rden[:, :, :].unsqueeze(3).to_broadcast([P, TU, HG, HD]),
                                      ALU.mult).then_inc(free, 1)
                if name in POST:
                    (t0, t1), n = tiles(u), unit_no[u[0:2]]
                    cols = slice(P * t0, P * t1)
                if name == "out":
                    src, free = side_ready(dve, st)
                    dve.wait_ge(s_xb, n + 1)
                    dve.tensor_tensor(x2[:, t0:t1], src[:, cols].rearrange("p (t d) -> p t d", d=D),
                                      xs[:, 2 * u[0] + u[1], t0:t1], ALU.add).then_inc(free, 1)
                    wait_read(dve, "out", u)
                    statistics(x2, nth(st, "nz", "ln"), t0, t1)
                if name == "ln":
                    normalise(xn2, x2, nth(("out", u), "norm1", "out"), t0, t1)
                if name == "rt":
                    src, free = side_ready(dve, st)
                    lg = src[:, NE * t0:NE * t1].rearrange("p (t e) -> p t e", e=NE)
                    top, eq = lmax[:, t0:t1], leq[:, t0:t1]
                    top_e = top.unsqueeze(2).to_broadcast([P, t1 - t0, NE])
                    dve.wait_ge(s_consts, 1)
                    link(dve.tensor_reduce(top, lg, AX.X, ALU.max))
                    link(dve.tensor_tensor(eq, lg, top_e, ALU.is_equal))
                    link(dve.tensor_tensor(eq, eq, rank[:, t0:t1], ALU.mult))
                    link(dve.tensor_reduce(top, eq, AX.X, ALU.max))
                    dve.tensor_tensor(onehot[:, t0:t1], eq, top_e, ALU.is_equal).then_inc(free, 1)
                if name[0] == "a":
                    c, i = int(name[1]), nth(st, *HIDDEN) % 2
                    wait_read(dve, name, u)
                    if n:
                        wait_read(dve, "y1", last_piece(n - 1))
                    dve.scalar_tensor_tensor(out=fg[:, c, cols], in0=fa[:, i, cols], scalar=0.5, in1=fa[:, i, cols],
                                             op0=ALU.mult, op1=ALU.max).then_inc(s_fl, 1)
                if name[0] == "m" and name[1:].isdigit():
                    c = int(name[1])
                    src, free = side_ready(dve, st)
                    dve.wait_ge(s_fs, squares.index((u, c)) + 1)
                    dve.tensor_tensor(fg[:, c, cols], src[:, cols], fg[:, c, cols], ALU.mult).then_inc(free, 1)
                if name in ("y0", "y1"):
                    src, free = side_ready(dve, st)
                    if name == "y0" and n:
                        dve.wait_ge(s_out, 16 * n)
                    if name == "y1":
                        wait_read(dve, "y0", u)
                    dve.tensor_tensor(y[:, t0:t1], src[:, cols].rearrange("p (t d) -> p t d", d=D),
                                      (x2 if name == "y0" else y)[:, t0:t1], ALU.add).then_inc(free, 1)

            dve.memset(ones[:, :], ONES).then_inc(s_one, 1)
            for half in range(2):
                last = dve.memset(tmax[half][:, :, 1], LOW)
            link(last)
            for st in PRE:
                run(st)
            for i in range(slots):
                if i in a_at:
                    s, (kind, r, h0, nh, nk) = a_at[i]
                    dve.wait_ge(s_a, i + 1)
                    src = ps_a[:, i % NA, 0:nh * nk].rearrange("p (h k) -> p h k", h=nh)
                    if s >= 2 and a_at[i - 1][0] != s:
                        dve.wait_ge(s_negm, s - 1)
                    dst = tmax[STEPS[s][1]][:, s % 2, ("diag", "tri", "sq").index(kind), r, h0:h0 + nh]
                    dve.tensor_reduce(dst, src, AX.X, ALU.max).then_inc(s_max, 1)
                for st in stages.get(i, []):
                    run(st)

        @block.tensor
        def _(pe):
            def fill(st, k=0):
                ap, i, use = side(st, k)
                if use:
                    pe.wait_ge(s_sfree[i], use)
                elif i >= 2:
                    pe.wait_ge(s_max, len(a_at))
                return ap, s_side[i]

            def run(st):
                name, u = st[0], st[1]
                if name == "mod":
                    pe.wait_ge(s_ldmod, 16)
                    pe.wait_ge(s_silu, 1)
                    dst, full_ = fill(st, 0)
                    for j, k in enumerate([0, 1, 3, 4]):
                        last = pe.matmul(dst[:, B * j:B * j + B], wmod_sb[:, D * k:D * k + D], silu[:, :],
                                         start=True, stop=True)
                    last.then_inc(full_, 1)
                if name == "gate":
                    dst, full_ = fill(st)
                    for b in range(B):
                        for j, k in enumerate([2, 5]):
                            c = (2 * b + j) * D
                            last = pe.matmul(dst[:, c:c + D], silu_b[:, b], wmod_sb[:, D * k:D * k + D],
                                             start=True, stop=True)
                    last.then_inc(full_, 1)
                t0, t1 = tiles(u) if name in POST else (0, TU)
                cols = slice(P * t0, P * t1)
                if name in ("hT", "h2"):
                    src = xn if name == "hT" else xn2
                    pe.wait_ge(s_ident, 1)
                    pe.wait_ge(s_xn, 1 + nth(("nz" if name == "hT" else "ln", u), "nz", "ln"))
                    dst, full_ = fill(st)
                    for t in range(t0, t1):
                        last = pe.transpose(dst[:, P * t:P * t + P], src[:, t], ident[:, :])
                    last.then_inc(full_, 1)
                if name in ("q1", "k1"):
                    i = (0, 1)[name == "k1"]
                    if i == 0:
                        pe.wait_ge(s_ldqkv, 64)
                    wait_read(pe, "hT", u)
                    for j, w in enumerate((wqkv_sb, wsw_sb)):
                        dst, full_ = fill(st, j)
                        pe.matmul(dst, w[:, D * i:D * i + D], ht[:, :], start=True, stop=True).then_inc(full_, 1)
                if name == "v":
                    dst, full_ = fill(st)
                    for t in range(TU):
                        last = pe.matmul(dst[:, D * t:D * t + D], ht[:, P * t:P * t + P], wqkv_sb[:, 2 * D:3 * D],
                                         start=True, stop=True)
                    last.then_inc(full_, 1)
                if name == "max2":
                    s = u
                    pe.wait_ge(s_negp, s + 1)
                    dst, full_ = fill(st)
                    pe.transpose(dst[0:PARTS * HG * TU, 0:P // 2].bitcast(BF16),
                                 negp[:, s % 2].rearrange("p c m -> p (c m)"), identb[:, :]).then_inc(full_, 1)
                if name[0] == "n" and name[1:].isdigit():
                    g = int(name[1])
                    pe.wait_ge(s_ot, NG * unit_no[u] + g + 1)
                    dst, full_ = fill(st)
                    for t in range(TU):
                        last = pe.transpose(dst[:, P * t:P * t + P], ot[:, g, P * t:P * t + P], ident[:, :])
                    last.then_inc(full_, 1)
                if name == "oT":
                    for g in range(NG):
                        wait_read(pe, f"n{g}", u[0:2])
                    dst, full_ = fill(st)
                    for t in range(t0, t1):
                        last = pe.transpose(dst[:, P * t:P * t + P], on[:, t], ident[:, :])
                    last.then_inc(full_, 1)
                if name == "out":
                    wait_read(pe, "oT", u)
                    pe.wait_ge(s_gated, 1)
                    dst, full_ = fill(st)
                    for t in range(t0, t1):
                        last = pe.matmul(dst[:, D * t:D * t + D], ont[:, P * t:P * t + P], wog[:, u[0]],
                                         start=True, stop=True)
                    last.then_inc(full_, 1)
                if name == "rt":
                    wait_read(pe, "h2", u)
                    dst, full_ = fill(st)
                    for t in range(t0, t1):
                        last = pe.matmul(dst[:, NE * t:NE * t + NE], h2t[:, P * t:P * t + P], wr_sb[:, :],
                                         start=True, stop=True)
                    last.then_inc(full_, 1)
                if name == "ohT":
                    wait_read(pe, "rt", u)
                    dst, full_ = fill(st)
                    for t in range(t0, t1):
                        last = pe.transpose(dst[0:NE, P * t:P * t + P], onehot[:, t], ident[:, :])
                    last.then_inc(full_, 1)
                if name[0] == "a":
                    c = int(name[1])
                    dst, full_ = fill(st)
                    pe.matmul(dst[:, cols], wfc_sb[:, P * c:P * c + P], h2t[:, cols], start=True, stop=True).then_inc(full_, 1)
                if name[0] == "m" and name[1:].isdigit():
                    c = int(name[1])
                    wait_read(pe, "ohT", u)
                    pe.wait_ge(s_consts, 1)
                    dst, full_ = fill(st)
                    pe.matmul(dst[:, cols], esel[:, P * c:P * c + P], oht[:, cols], start=True, stop=True).then_inc(full_, 1)
                if name in ("y0", "y1"):
                    c1 = 1 if name == "y0" else 3
                    dst, full_ = fill(st)
                    wait_read(pe, f"m{c1}", u)
                    for t in range(t0, t1):
                        for c in (c1 - 1, c1):
                            last = pe.matmul(dst[:, D * t:D * t + D], fg[:, c, P * t:P * t + P], wpg[:, u[0], c],
                                             start=(c < c1), stop=(c == c1))
                    last.then_inc(full_, 1)

            def keep_warm(n, to=ps_a):
                for _ in range(n):
                    pe.matmul(to[:, 0, :], identb[:, :], maska[:, :, :].rearrange("p h k -> p (h k)"),
                              start=True, stop=True)

            def stack_ready(s):
                b, half, g = STEPS[s]
                for hf in ((0, 1) if half or b else (0,)):
                    pe.wait_ge(s_stack[hf][g], 2 * 16 * (b + 1))

            def pass_a(i):
                s, (kind, r, h0, nh, nk) = a_at[i]
                b, half, g = STEPS[s]
                if i == 0 or a_at[i - 1][0] != s:
                    stack_ready(s)
                if i >= NA:
                    pe.wait_ge(s_max, i - NA + 1)
                dst = ps_a[:, i % NA, :]
                if kind == "diag":
                    pe.matmul(dst, identb[:, :], maska[:, :, :].rearrange("p h k -> p (h k)"), start=True, stop=False,
                              skip_group_check=True)
                for j in range(nh):
                    h = HG * g + h0 + j
                    k0, kh = (r * P, half) if kind == "diag" else (0, half) if kind == "tri" else (0, 0)
                    last = pe.matmul(dst[:, j * nk:(j + 1) * nk], qst[0:ROWS, half, h, r * P:r * P + P],
                                     kst[0:ROWS, kh, h, k0:k0 + nk], start=(kind != "diag"), stop=True,
                                     skip_group_check=True)
                last.then_inc(s_a, 1)

            def pass_b(i):
                s, gi, (kt, kh, c0, _), (h0, nh), _ = b_at[i]
                b, half, g = STEPS[s]
                n, w = bank_no[i], HALF - c0
                if n == 0:
                    pe.wait_ge(s_ones, 1)
                if gi == 0 and h0 == 0:
                    pe.wait_ge(s_mstack[s % 2], 48 * (s // 2 + 1))
                if n >= 2:
                    pe.wait_ge(s_exp, n - 1)
                for j in range(nh):
                    h = HG * g + h0 + j
                    last = pe.matmul(ps_b[:, n % 2, j * w:(j + 1) * w], kst[:, kh, h, kt * P:kt * P + P],
                                     qst[:, half, h, c0:HALF], start=True, stop=True)
                last.then_inc(s_b, 1)

            def times_v(s, gi, grp):
                kt, kh, c0, banks = grp
                b, half, g = STEPS[s]
                G, n = group_no[(s, gi)], len(groups_b(half))
                pe.wait_ge(s_exp, max(bank_no[i] for i in b_at if b_at[i][0:2] == (s, gi)) + 1)
                diagonal = gi >= n - TU
                if diagonal:
                    pe.wait_ge(s_tri, TU * s + gi - (n - TU) + 1)
                if gi == 0 and s:
                    pe.wait_ge(s_ot, s)
                if gi == 0:
                    pe.wait_ge(s_vones, 1)
                    wait_read(pe, "v", (b, 1) if half or b else (b, 0))
                for j in range(HG):
                    c = (HG * g + j) * VW
                    last = pe.matmul(ps_o[32 * j:32 * j + 32, 0, c0:HALF], v_sb[:, TU * (2 * b + kh) + kt, c:c + 32],
                                     pt[:, G % NP, j, 0:HALF - c0], start=(gi == 0), stop=(gi == n - 1))
                last.then_inc(s_pv, 1)

            pe.wait_ge(s_mask, 1)
            keep_warm(WARM_PRE["start"])
            for st in PRE:
                run(st)
                keep_warm(WARM_PRE.get(st[0], 0) if st[1] in (0, (0, 0)) else 0)
            for i in range(slots):
                if i in a_at:
                    pass_a(i)
                if i in b_at:
                    pass_b(i)
                if i < min(b_at):
                    keep_warm(1, ps_b)
                if i in v_at:
                    times_v(*v_at[i])
                if i > max(a_at) and i in b_at:
                    if i == max(a_at) + 1:
                        pe.wait_ge(s_max, len(a_at))
                    keep_warm(1)
                for st in pe_at.get(i, []):
                    run(st)
                    if i > max(b_at) and st[0] in WARM_POST:
                        if st[0] == "n3":
                            pe.wait_ge(s_max, len(a_at))
                        if st[0] == "n3" or st[1] == last_piece(len(UNITS) - 1):
                            keep_warm(WARM_POST[st[0]])


def rope_tables():
    import numpy as np
    inv = (1.0 / 10000.0 ** (np.arange(0, HD, 2, dtype=np.float32) / np.float32(HD))).astype(np.float32)
    f = np.arange(T, dtype=np.float32)[:, None] * inv[None, :]
    r = np.concatenate([np.sin(f), np.cos(f)], axis=-1).astype(np.float32)
    sin, cos = r[:, ::2], r[:, 1::2]
    c = np.repeat(cos, 2, axis=1)
    s = np.stack([-sin, sin], axis=-1).reshape(T, HD)
    return np.stack([np.repeat(c.T, H, axis=0), np.repeat(s.T, H, axis=0)], axis=1)


def kernel(**inputs):
    import numpy as np
    import concourse.bacc as bacc
    from concourse.bass_utils import run_bass_kernel_spmd as run

    a = {k[3:]: np.asarray(v) for k, v in inputs.items()}
    dh = np.arange(D).reshape(H, HD).T.ravel()
    qk = np.concatenate([dh, D + dh])
    qkv_w, qkv_b = a["attn_qkv_w"], a["attn_qkv_b"]
    bq, bs = qkv_b[qk], qkv_b[qk ^ 1]
    data = {
        "x": a["attn_x"].reshape(B * 2, TU, P, D).transpose(0, 2, 1, 3),
        "ct": a["c"].T,
        "wmod": a["wmod"],
        "wqkv": np.concatenate([qkv_w[:, qk], qkv_w[:, 2 * D:]], axis=1),
        "wsw": qkv_w[:, qk ^ 1],
        "bcol": np.stack([bq[:D], bs[:D], bq[D:], bs[D:]], axis=1),
        "bv": qkv_b[2 * D:],
        "wo": a["attn_out_w"],
        "bo": a["attn_out_b"],
        "wr": a["ffn_w_router"].T,
        "wfc": a["ffn_w_fc"].reshape(HID, D).T,
        "wpj": a["ffn_w_proj"].transpose(0, 2, 1).reshape(4, P, D).transpose(1, 0, 2),
        "rope": rope_tables(),
    }
    data = {f"in_{k}": np.ascontiguousarray(v) for k, v in data.items()}
    nc = bacc.Bacc("TRN2", target_bir_lowering=False, num_devices=1)
    args = [nc.dram_tensor(k, v.shape, mybir.dt.from_np(v.dtype), kind="ExternalInput").ap() for k, v in data.items()]
    out = nc.dram_tensor("out", (B * 2, P, TU, D), F32, kind="ExternalOutput").ap()
    adaln_block(nc, *args, out)
    got = run(nc, [data], core_ids=[0]).results[0]["out"]
    return got.transpose(0, 2, 1, 3).reshape(B, T, D)
```
